# Optimizing a Trainium2 kernel written in Bass

```python
import numpy as np
import jax
import jax.numpy as jnp

def _softmax(x, axis=-1):
    return jax.nn.softmax(x, axis=axis)

def _gelu(x):
    return jax.nn.gelu(x, approximate=True)

def _silu(x):
    return jax.nn.silu(x)

def _sigmoid(x):
    return jax.nn.sigmoid(x)

def _layernorm(x, axis=-1, eps=1e-05):
    m = jnp.mean(x, axis=axis, keepdims=True)
    v = jnp.var(x, axis=axis, keepdims=True)
    return (x - m) / jnp.sqrt(v + eps)

def _scatter_add(tgt, idx, src, axis=0):
    return tgt.at[idx].add(src)

def _segment_sum(src, seg, n):
    return jax.ops.segment_sum(src, seg, n)
kernel_name = 'mk_xattn_ffn_d2_seqx_r8_e6d2ce'

def setup_inputs(seed: int=0):
    np.random.seed(seed)
    _w = jnp.asarray

    def _rec_inputs():
        import jax
        import jax.numpy as jnp
        _rk = jax.random.key(seed)
        x = -0.0003929 + 0.9999 * jax.random.normal(jax.random.fold_in(_rk, 1), (32, 56, 128), jnp.float32)
        _lenS = 56 - jax.random.randint(jax.random.fold_in(_rk, 7), (32,), 0, max(1, 56 // 4) + 1, jnp.int32)
        _lenS2 = 1500 - jax.random.randint(jax.random.fold_in(_rk, 8), (32,), 0, max(1, 1500 // 4) + 1, jnp.int32)
        _ctx_1024P = jax.random.normal(jax.random.fold_in(_rk, 11), (32, 16, 128), jnp.float32)
        _ctx_1024c = jax.random.dirichlet(jax.random.fold_in(_rk, 511), 0.3 * jnp.ones((16,), jnp.float32), (32, 1500))
        _ctx_1024t = jnp.einsum('bsk,bkd->bsd', _ctx_1024c, _ctx_1024P)
        _ctx_1024t = _ctx_1024t * jax.lax.rsqrt(jnp.mean(jnp.square(_ctx_1024t)) + 1e-12) * 0.953939
        ctx_1024 = 4.13588e-05 + 0.999923 * (_ctx_1024t + 0.3 * jax.random.normal(jax.random.fold_in(_rk, 611), (32, 1500, 128), jnp.float32))
        _validS = jnp.arange(56)[None, :] < _lenS[:, None]
        _validS2 = jnp.arange(1500)[None, :] < _lenS2[:, None]
        _causal = jnp.tril(jnp.ones((56, 56), dtype=bool))
        mask_1xSxS2_bk0 = jnp.logical_not(jnp.broadcast_to(_validS2[0:1, None, :], (1, 56, 1500)))
        return (x, ctx_1024, mask_1xSxS2_bk0)
    x, ctx_1024, mask_1xSxS2_bk0 = _rec_inputs()

    def _L0_xattn_setup():
        import jax, jax.numpy as jnp
        import numpy as np
        H = 128
        B = 8
        L_CHAR = 256
        L_SUB = 128

        def _linear(x, W, b):
            return jnp.einsum('blh,oh->blo', x, W) + b

        def _interp_linear(x, out_len):
            L_in = x.shape[1]
            pos = (jnp.arange(out_len, dtype=x.dtype) + 0.5) * (L_in / out_len) - 0.5
            pos = jnp.clip(pos, 0.0, L_in - 1)
            lo = jnp.floor(pos).astype(jnp.int32)
            hi = jnp.minimum(lo + 1, L_in - 1)
            w = (pos - lo.astype(x.dtype))[None, :, None]
            return x[:, lo] * (1 - w) + x[:, hi] * w
        key = jax.random.key(seed)
        ks = jax.random.split(key, 18)
        s = 0.02
        inp = {'char_emb': jax.random.normal(ks[0], (B, L_CHAR, H), jnp.float32), 'subword_emb': jax.random.normal(ks[1], (B, L_SUB, H), jnp.float32)}
        names = ['Wq_c', 'Wk_s', 'Wv_s', 'Wq_s', 'Wk_c', 'Wv_c']
        for i, n in enumerate(names):
            inp[n] = jax.random.normal(ks[2 + 2 * i], (H, H), jnp.float32) * s
            inp['b' + n[1:]] = jax.random.normal(ks[3 + 2 * i], (H,), jnp.float32) * s
        inp['Wg'] = jax.random.normal(ks[14], (H, 2 * H), jnp.float32) * s
        inp['bg'] = jax.random.normal(ks[15], (H,), jnp.float32) * s
        return inp
    _L0_xattn_all = _L0_xattn_setup()
    _L0_xattn_in = {k: v for k, v in _L0_xattn_all.items() if k in ('Wq_c', 'bq_c', 'Wk_s', 'bk_s', 'Wv_s', 'bv_s', 'Wq_s', 'bq_s', 'Wk_c', 'bk_c', 'Wv_c', 'bv_c', 'Wg', 'bg')}
    del _L0_xattn_all

    def _L0_ffn_setup():
        import jax, jax.numpy as jnp
        import numpy as np
        DIM = 128
        INTER = 128
        N_EXPERTS = 8
        TOPK = 2
        N_SHARED = 2
        key = jax.random.key(seed)
        ks = jax.random.split(key, 10)
        s = 0.02
        return {'x': jax.random.normal(ks[0], (4, 256, DIM), dtype=jnp.float32), 'gate_w': jax.random.normal(ks[1], (N_EXPERTS, DIM), dtype=jnp.float32) * s, 'gate_bias': jax.random.normal(ks[2], (N_EXPERTS,), dtype=jnp.float32) * s, 'w1': jax.random.normal(ks[3], (N_EXPERTS, INTER, DIM), dtype=jnp.float32) * s, 'w3': jax.random.normal(ks[4], (N_EXPERTS, INTER, DIM), dtype=jnp.float32) * s, 'w2': jax.random.normal(ks[5], (N_EXPERTS, DIM, INTER), dtype=jnp.float32) * s, 'sw1': jax.random.normal(ks[6], (N_SHARED * INTER, DIM), dtype=jnp.float32) * s, 'sw3': jax.random.normal(ks[7], (N_SHARED * INTER, DIM), dtype=jnp.float32) * s, 'sw2': jax.random.normal(ks[8], (DIM, N_SHARED * INTER), dtype=jnp.float32) * s}
    _L0_ffn_all = _L0_ffn_setup()
    _L0_ffn_in = {k: v for k, v in _L0_ffn_all.items() if k in ('gate_w', 'gate_bias', 'w1', 'w3', 'w2', 'sw1', 'sw3', 'sw2')}
    del _L0_ffn_all

    def _L1_xattn_setup():
        import jax, jax.numpy as jnp
        import numpy as np
        B, S, D = (4, 256, 128)
        key = jax.random.key(seed)
        kv, kk, kq, kw = jax.random.split(key, 4)
        scale = 1.0 / np.sqrt(D)
        v = jax.random.normal(kv, (B, S, D), dtype=jnp.float32)
        k = jax.random.normal(kk, (B, S, D), dtype=jnp.float32)
        q = jax.random.normal(kq, (B, S, D), dtype=jnp.float32)
        wi = jax.random.normal(kw, (D, D), dtype=jnp.float32) * scale
        mask = jnp.tril(jnp.ones((S, S), dtype=bool))[None, :, :]
        return {'v': v, 'k': k, 'q': q, 'wi': wi, 'mask': mask}
    _L1_xattn_all = _L1_xattn_setup()
    _L1_xattn_in = {k: v for k, v in _L1_xattn_all.items() if k in ('wi',)}
    del _L1_xattn_all

    def _L1_ffn_setup():
        import jax, jax.numpy as jnp
        import numpy as np
        HIDDEN_SIZE = 128
        NUM_EXPERTS = 8
        MOE_INTERMEDIATE_SIZE = 176
        NUM_EXPERTS_PER_TOK = 2
        SHARED_EXPERT_INTERMEDIATE_SIZE = 352
        B, T = (2, 128)
        W_SCALE = 0.02
        key = jax.random.key(seed)
        ks = jax.random.split(key, 8)
        H, E, I, SI = (HIDDEN_SIZE, NUM_EXPERTS, MOE_INTERMEDIATE_SIZE, SHARED_EXPERT_INTERMEDIATE_SIZE)
        return {'x': jax.random.normal(ks[0], (B, T, H), jnp.float32), 'gate_w': jax.random.normal(ks[1], (E, H), jnp.float32) * W_SCALE, 'experts_gate_up': jax.random.normal(ks[2], (E, 2 * I, H), jnp.float32) * W_SCALE, 'experts_down': jax.random.normal(ks[3], (E, H, I), jnp.float32) * W_SCALE, 'shared_gate_w': jax.random.normal(ks[4], (SI, H), jnp.float32) * W_SCALE, 'shared_up_w': jax.random.normal(ks[5], (SI, H), jnp.float32) * W_SCALE, 'shared_down_w': jax.random.normal(ks[6], (H, SI), jnp.float32) * W_SCALE, 'shared_expert_gate_w': jax.random.normal(ks[7], (1, H), jnp.float32) * W_SCALE}
    _L1_ffn_all = _L1_ffn_setup()
    _L1_ffn_in = {k: v for k, v in _L1_ffn_all.items() if k in ('gate_w', 'experts_gate_up', 'experts_down', 'shared_gate_w', 'shared_up_w', 'shared_down_w', 'shared_expert_gate_w')}
    del _L1_ffn_all
    return {'x': x, 'ctx_1024': ctx_1024, 'mask_1xSxS2_bk0': mask_1xSxS2_bk0, 'L0_xattn_Wq_c': _L0_xattn_in['Wq_c'], 'L0_xattn_bq_c': _L0_xattn_in['bq_c'], 'L0_xattn_Wk_s': _L0_xattn_in['Wk_s'], 'L0_xattn_bk_s': _L0_xattn_in['bk_s'], 'L0_xattn_Wv_s': _L0_xattn_in['Wv_s'], 'L0_xattn_bv_s': _L0_xattn_in['bv_s'], 'L0_xattn_Wq_s': _L0_xattn_in['Wq_s'], 'L0_xattn_bq_s': _L0_xattn_in['bq_s'], 'L0_xattn_Wk_c': _L0_xattn_in['Wk_c'], 'L0_xattn_bk_c': _L0_xattn_in['bk_c'], 'L0_xattn_Wv_c': _L0_xattn_in['Wv_c'], 'L0_xattn_bv_c': _L0_xattn_in['bv_c'], 'L0_xattn_Wg': _L0_xattn_in['Wg'], 'L0_xattn_bg': _L0_xattn_in['bg'], 'L0_ffn_gate_w': _L0_ffn_in['gate_w'], 'L0_ffn_gate_bias': _L0_ffn_in['gate_bias'], 'L0_ffn_w1': _L0_ffn_in['w1'], 'L0_ffn_w3': _L0_ffn_in['w3'], 'L0_ffn_w2': _L0_ffn_in['w2'], 'L0_ffn_sw1': _L0_ffn_in['sw1'], 'L0_ffn_sw3': _L0_ffn_in['sw3'], 'L0_ffn_sw2': _L0_ffn_in['sw2'], 'L1_xattn_wi': _L1_xattn_in['wi'], 'L1_ffn_gate_w': _L1_ffn_in['gate_w'], 'L1_ffn_experts_gate_up': _L1_ffn_in['experts_gate_up'], 'L1_ffn_experts_down': _L1_ffn_in['experts_down'], 'L1_ffn_shared_gate_w': _L1_ffn_in['shared_gate_w'], 'L1_ffn_shared_up_w': _L1_ffn_in['shared_up_w'], 'L1_ffn_shared_down_w': _L1_ffn_in['shared_down_w'], 'L1_ffn_shared_expert_gate_w': _L1_ffn_in['shared_expert_gate_w']}

def reference(x, ctx_1024, mask_1xSxS2_bk0, L0_xattn_Wq_c, L0_xattn_bq_c, L0_xattn_Wk_s, L0_xattn_bk_s, L0_xattn_Wv_s, L0_xattn_bv_s, L0_xattn_Wq_s, L0_xattn_bq_s, L0_xattn_Wk_c, L0_xattn_bk_c, L0_xattn_Wv_c, L0_xattn_bv_c, L0_xattn_Wg, L0_xattn_bg, L0_ffn_gate_w, L0_ffn_gate_bias, L0_ffn_w1, L0_ffn_w3, L0_ffn_w2, L0_ffn_sw1, L0_ffn_sw3, L0_ffn_sw2, L1_xattn_wi, L1_ffn_gate_w, L1_ffn_experts_gate_up, L1_ffn_experts_down, L1_ffn_shared_gate_w, L1_ffn_shared_up_w, L1_ffn_shared_down_w, L1_ffn_shared_expert_gate_w):
    import jax
    import jax.numpy as jnp

    def _L0_xattn_ref(char_emb, subword_emb, Wq_c, bq_c, Wk_s, bk_s, Wv_s, bv_s, Wq_s, bq_s, Wk_c, bk_c, Wv_c, bv_c, Wg, bg):
        import jax, jax.numpy as jnp
        import numpy as np
        H = 128
        B = 8
        L_CHAR = 256
        L_SUB = 128

        def _linear(x, W, b):
            return jnp.einsum('blh,oh->blo', x, W) + b

        def _interp_linear(x, out_len):
            L_in = x.shape[1]
            pos = (jnp.arange(out_len, dtype=x.dtype) + 0.5) * (L_in / out_len) - 0.5
            pos = jnp.clip(pos, 0.0, L_in - 1)
            lo = jnp.floor(pos).astype(jnp.int32)
            hi = jnp.minimum(lo + 1, L_in - 1)
            w = (pos - lo.astype(x.dtype))[None, :, None]
            return x[:, lo] * (1 - w) + x[:, hi] * w
        h = char_emb.shape[-1]
        scale = 1.0 / jnp.sqrt(jnp.asarray(h, char_emb.dtype))
        Q_char = _linear(char_emb, Wq_c, bq_c)
        K_sub = _linear(subword_emb, Wk_s, bk_s)
        V_sub = _linear(subword_emb, Wv_s, bv_s)
        scores = jnp.einsum('bqh,bkh->bqk', Q_char, K_sub) * scale
        char2sub = jnp.einsum('bqk,bkh->bqh', jax.nn.softmax(scores, axis=-1), V_sub)
        Q_sub = _linear(subword_emb, Wq_s, bq_s)
        K_char = _linear(char_emb, Wk_c, bk_c)
        V_char = _linear(char_emb, Wv_c, bv_c)
        scores2 = jnp.einsum('bqh,bkh->bqk', Q_sub, K_char) * scale
        sub2char = jnp.einsum('bqk,bkh->bqh', jax.nn.softmax(scores2, axis=-1), V_char)
        L_char = char_emb.shape[1]
        if sub2char.shape[1] != L_char:
            sub2char = _interp_linear(sub2char, L_char)
        gate_in = jnp.concatenate([char2sub, sub2char], axis=-1)
        gate = jax.nn.sigmoid(jnp.einsum('blh,oh->blo', gate_in, Wg) + bg)
        return gate * char2sub + (1 - gate) * sub2char

    def _L0_ffn_ref(x, gate_w, gate_bias, w1, w3, w2, sw1, sw3, sw2):
        import jax, jax.numpy as jnp
        import numpy as np
        DIM = 128
        INTER = 128
        N_EXPERTS = 8
        TOPK = 2
        N_SHARED = 2
        shape = x.shape
        xt = x.reshape(-1, shape[-1])
        scores = jax.nn.softmax((xt @ gate_w.T).astype(jnp.float32), axis=-1)
        _, idx = jax.lax.top_k(scores + gate_bias, TOPK)
        weights = jnp.take_along_axis(scores, idx, axis=1).astype(x.dtype)
        y = jnp.zeros_like(xt)
        for e in range(N_EXPERTS):
            gate_e = jnp.sum(jnp.where(idx == e, weights, 0.0), axis=1)
            h = jax.nn.silu(xt @ w1[e].T) * (xt @ w3[e].T)
            y = y + gate_e[:, None] * (h @ w2[e].T)
        z = jax.nn.silu(xt @ sw1.T) * (xt @ sw3.T) @ sw2.T
        return (y + z).reshape(shape)

    def _L1_xattn_ref(v, k, q, wi, mask):
        import jax, jax.numpy as jnp
        import numpy as np
        B, S, D = (4, 256, 128)
        q = q @ wi
        k = k @ wi
        v = v @ wi
        scores = jnp.einsum('bqd,bkd->bqk', q, k) / jnp.sqrt(jnp.asarray(q.shape[-1], q.dtype))
        scores = jnp.where(mask, scores, jnp.asarray(-10000000000.0, scores.dtype))
        attn = jax.nn.softmax(scores, axis=-1)
        return q + jnp.einsum('bqk,bkd->bqd', attn, v)

    def _L1_ffn_ref(x, gate_w, experts_gate_up, experts_down, shared_gate_w, shared_up_w, shared_down_w, shared_expert_gate_w):
        import jax, jax.numpy as jnp
        import numpy as np
        HIDDEN_SIZE = 128
        NUM_EXPERTS = 8
        MOE_INTERMEDIATE_SIZE = 176
        NUM_EXPERTS_PER_TOK = 2
        SHARED_EXPERT_INTERMEDIATE_SIZE = 352
        B, T = (2, 128)
        W_SCALE = 0.02
        Bx, Tx, H = x.shape
        E = gate_w.shape[0]
        I = experts_down.shape[2]
        x_flat = x.reshape(Bx * Tx, H)
        logits = x_flat @ gate_w.T
        scores = jax.nn.softmax(logits, axis=-1)
        _, topk_ids = jax.lax.top_k(scores, NUM_EXPERTS_PER_TOK)
        in_topk = jax.nn.one_hot(topk_ids, E, dtype=x.dtype).sum(axis=1)
        w = scores * in_topk
        gu = jnp.einsum('nh,eih->nei', x_flat, experts_gate_up)
        g, u = (gu[..., :I], gu[..., I:])
        h = jax.nn.silu(g) * u
        expert_out = jnp.einsum('nei,ehi->neh', h, experts_down)
        out = jnp.einsum('neh,ne->nh', expert_out, w)
        shared = jax.nn.silu(x_flat @ shared_gate_w.T) * (x_flat @ shared_up_w.T) @ shared_down_w.T
        shared_weight = jax.nn.sigmoid(x_flat @ shared_expert_gate_w.T)
        out = out + shared_weight * shared
        return out.reshape(Bx, Tx, H)
    x = x + _L0_xattn_ref(_layernorm(x, axis=-1), ctx_1024, L0_xattn_Wq_c, L0_xattn_bq_c, L0_xattn_Wk_s, L0_xattn_bk_s, L0_xattn_Wv_s, L0_xattn_bv_s, L0_xattn_Wq_s, L0_xattn_bq_s, L0_xattn_Wk_c, L0_xattn_bk_c, L0_xattn_Wv_c, L0_xattn_bv_c, L0_xattn_Wg, L0_xattn_bg)
    x = x + _L0_ffn_ref(_layernorm(x, axis=-1), L0_ffn_gate_w, L0_ffn_gate_bias, L0_ffn_w1, L0_ffn_w3, L0_ffn_w2, L0_ffn_sw1, L0_ffn_sw3, L0_ffn_sw2)
    x = x + _L1_xattn_ref(ctx_1024, ctx_1024, _layernorm(x, axis=-1), L1_xattn_wi, mask_1xSxS2_bk0)
    x = x + _L1_ffn_ref(_layernorm(x, axis=-1), L1_ffn_gate_w, L1_ffn_experts_gate_up, L1_ffn_experts_down, L1_ffn_shared_gate_w, L1_ffn_shared_up_w, L1_ffn_shared_down_w, L1_ffn_shared_expert_gate_w)
    return x

_drawn_inputs = setup_inputs


def setup_inputs(seed=0):
    import zlib

    import numpy as np

    out = dict(_drawn_inputs(seed))
    spreads = {}
    factors = {'L0_xattn_Wq_c': 8.0,
     'L0_xattn_bq_c': 8.0,
     'L0_xattn_Wk_s': 8.0,
     'L0_xattn_bk_s': 8.0,
     'L0_xattn_bv_s': 5.552,
     'L0_xattn_Wq_s': 8.0,
     'L0_xattn_bq_s': 8.0,
     'L0_xattn_Wk_c': 8.0,
     'L0_xattn_bk_c': 8.0,
     'L0_xattn_Wv_c': 4.053,
     'L0_xattn_bv_c': 5.508,
     'L0_xattn_Wg': 8.0,
     'L0_xattn_bg': 8.0,
     'L0_ffn_gate_w': 8.0,
     'L0_ffn_gate_bias': 8.0,
     'L0_ffn_w1': 8.0,
     'L0_ffn_w3': 8.0,
     'L0_ffn_w2': 8.0,
     'L0_ffn_sw1': 7.213,
     'L0_ffn_sw3': 7.138,
     'L0_ffn_sw2': 7.141,
     'L1_ffn_gate_w': 8.0,
     'L1_ffn_experts_gate_up': 8.0,
     'L1_ffn_experts_down': 8.0,
     'L1_ffn_shared_gate_w': 8.0,
     'L1_ffn_shared_up_w': 8.0,
     'L1_ffn_shared_down_w': 8.0,
     'L1_ffn_shared_expert_gate_w': 8.0}
    for name, (base, spread) in spreads.items():
        noise = np.random.default_rng([zlib.crc32(name.encode()), seed]).standard_normal(out[name].shape)
        drawn = base * np.exp(spread * noise) if base else spread * noise
        out[name] = jnp.asarray(drawn.astype(out[name].dtype))
    for name, factor in factors.items():
        out[name] = (out[name] * factor).astype(out[name].dtype)
    return out
```

```python
from contextlib import ExitStack

import concourse.bass as bass
from concourse import mybir

F32 = mybir.dt.float32
BF16 = mybir.dt.bfloat16
U8 = mybir.dt.uint8
ALU = mybir.AluOpType
ACT = mybir.ActivationFunctionType
X = mybir.AxisListType.X

BATCH, S, D, S2 = 32, 56, 128, 1500
HALF = 64
PAIR = 2 * HALF
PAIRS = 4
GROUPS = BATCH // (2 * PAIRS)
GT = PAIRS * PAIR
GR = PAIRS * 2 * S
BLOCKS = 12
BR = S2 // BLOCKS
MAIN = 112
BANK = 512
CHUNK = S2 // 3
E = 8
EPS = 1e-5
SCALE = float(D) ** -0.5
MASKED = -1e10
LOWEST = -3.0e38

L0_TILES = E + 2
I1, SI1 = 176, 352
L1_ROWS = E * I1 + SI1
L1_TILES = -(-L1_ROWS // 128)
L1_ROUTED = E * I1 // 128
GATE_ROWS = 96

W_NAMES = ["WqcT", "Wks", "WvsT", "WqsT", "WkcT", "WvcT", "WgaT", "WgbT", "wi", "wiT", "ident"]
B_NAMES = ["bq_c", "bk_c", "bq_s", "bv_s", "bg", "bk_s"]

RING = [3, 4, 5]
G_BANKS, U_BANKS, Y_BANK = [0, 1], [2, 7], 6


def ring_order():
    order = ["xnA", "q", "qk", "kc", "vc", "sel0", "sel1", "qs0", "qs1"]
    after = {0: ["s20", "s21"], 1: ["p2"], 2: ["s2c"], 3: []}
    for s in range(PAIRS):
        order += after[s] + [f"ptA{s}.{c}" for c in range(3)]
    order += ["onA", "c2s", "gate", "dx"]
    order += ["xnB", "lgB", "gtB"] + [f"gB{t}" for t in range(E)] + ["yB"]
    order += ["xnC", "q1", "qw"] + [f"ptC{s}.{c}" for s in range(PAIRS) for c in range(3)] + ["onC", "o1"]
    order += ["xnD", "lgD", "gtD"] + [f"gD{t}" for t in range(L1_TILES)] + ["yD"]
    return order


ORDER = ring_order()
AT = {name: k for k, name in enumerate(ORDER)}
FILLS = len(ORDER)
NORMS = 4
N_ZEROED = 7
N_SETUP = 7
DVE_STEPS = 79
USES = [len(range(b, FILLS, 3)) for b in range(3)]


def interpolation():
    import numpy as np
    one = np.float32
    pos = (np.arange(S, dtype=one) + one(0.5)) * one(S2 / S) - one(0.5)
    pos = np.clip(pos, one(0), one(S2 - 1)).astype(one)
    lo = np.floor(pos).astype(np.int32)
    hi = np.minimum(lo + 1, S2 - 1)
    return lo, hi, (pos - lo.astype(one)).astype(one)


def build(nc, d):
    with ExitStack() as ctx:
        def sb(name, shape, dt=F32):
            return ctx.enter_context(nc.sbuf_tensor(name, shape, dt))

        def sem(name):
            return ctx.enter_context(nc.semaphore(name))

        w = sb("w", [128, len(W_NAMES), D])
        W = {n: w[:, i, :] for i, n in enumerate(W_NAMES)}
        bias = sb("bias", [128, len(B_NAMES)])
        Bc = {n: bias[:, i:i + 1] for i, n in enumerate(B_NAMES)}
        neg_bg = sb("neg_bg", [128, 1])
        bv_c_row = sb("bv_c_row", [128, D])
        gate_bias = sb("gate_bias", [128, E])
        router = sb("router", [128, 2 * E + 1])
        up0 = sb("up0", [128, 2, L0_TILES * 128])
        down0 = sb("down0", [128, L0_TILES, D])
        up1 = sb("up1", [128, 2, L1_ROWS])
        down1 = sb("down1", [128, L1_TILES, D])
        spread0 = sb("spread0", [GATE_ROWS, E, 128], BF16)
        spread1 = sb("spread1", [GATE_ROWS, L1_TILES, 128], BF16)
        identb = sb("identb", [128, 128], BF16)
        before = sb("before", [128, E, E])
        w_interp = sb("w_interp", [128, PAIRS * 2])
        penalty = sb("penalty", [128, 3, CHUNK])
        any_col = sb("any_col", [128, 1])
        any_diag = sb("any_diag", [HALF, HALF])
        ones = sb("ones", [HALF, 128])
        any_row = sb("any_row", [128, HALF])
        minus_half = sb("minus_half", [128, PAIRS])

        rows = sb("rows", [128, PAIRS, 2, BLOCKS, D])
        cols = sb("cols", [128, PAIRS, 2, BLOCKS, BR])
        sel = sb("sel", [128, PAIRS, 2, D])
        x_in = sb("x_in", [128, PAIRS, D])
        x = sb("x", [128, PAIRS, D])
        x_out = sb("x_out", [128, PAIRS, D])
        stats = sb("stats", [128, PAIRS, 6])
        mv = sb("mv", [128, PAIRS, 2])
        var = sb("var", [128, PAIRS])
        rstd = sb("rstd", [128, PAIRS])
        xn = sb("xn", [128, PAIRS, D])
        xnT = sb("xnT", [128, GT])
        qT = sb("qT", [128, GT])
        qk = sb("qk", [128, GT])
        kcT = sb("kcT", [128, GT])
        vc = sb("vc", [128, PAIRS, D])
        late = sb("late", [128, 4, GT])
        selT = late[:, 0:2, :].rearrange("p a b -> p (a b)")
        qsT = late[:, 2:4, :].rearrange("p a (k t) -> p (a k) t", k=4)
        onT, c2sT, gate, diff = (late[:, i, :] for i in range(4))
        above, tied = (late[:, i, 0:PAIRS * E * E].rearrange("p (s e j) -> p s e j", s=PAIRS, e=E) for i in (1, 2))
        mask_u8 = late[:, 3, :].bitcast(U8)[:, 0:S2]
        s2 = sb("s2", [128, PAIRS * 2, S])
        s2max = sb("s2max", [128, PAIRS * 2])
        s2sum = sb("s2sum", [128, PAIRS * 2])
        coef = sb("coef", [128, PAIRS * 2])
        p2 = sb("p2", [128, PAIRS, PAIR])
        p2T = sb("p2T", [128, GT])
        s2cT = sb("s2cT", [128, GT])
        top = sb("top", [128, PAIRS])
        ntop = sb("ntop", [128, PAIRS])
        total = sb("total", [128, PAIRS])
        rtotal = sb("rtotal", [128, PAIRS])
        work = sb("work", [128, S2 + BLOCKS * PAIR])
        prob = work[:, 0:S2].rearrange("p (c n) -> p c n", c=3)
        pT = work[:, S2:S2 + BLOCKS * PAIR].rearrange("p (j t) -> p j t", j=BLOCKS)
        sg, hu, h = (work[:, i * 2 * GR:(i + 1) * 2 * GR].rearrange("p (k t) -> p k t", k=2) for i in range(3))
        on = sb("on", [128, PAIRS, D])
        lg = sb("lg", [128, PAIRS, E + 1])
        lmax = sb("lmax", [128, PAIRS])
        lsum = sb("lsum", [128, PAIRS])
        key = sb("key", [128, PAIRS, E])
        rank = sb("rank", [128, PAIRS, E])
        gates = sb("gates", [128, PAIRS, E + 1])
        rest = sb("rest", [128, PAIRS, E + 1])
        gates3 = sb("gates3", [128, PAIRS, GATE_ROWS], BF16)
        gatesT = sb("gatesT", [GATE_ROWS, GT], BF16)
        yT = sb("yT", [128, GT])

        ps = ctx.enter_context(nc.psum_tensor("ps", [128, 8, BANK], F32))

        def ring(name):
            return ps[:, RING[AT[name] % 3], :]

        scores = ps[:, 0:3, 0:CHUNK]

        w_in = sem("w_in")
        mask_in = sem("mask_in")
        experts_in = sem("experts_in")
        x_loaded, x_taken = sem("x_loaded"), sem("x_taken")
        sel_loaded = sem("sel_loaded")
        rows_loaded = [sem(f"rows_loaded{s}") for s in range(PAIRS)]
        cols_loaded = [sem(f"cols_loaded{s}") for s in range(PAIRS)]
        zeroed = sem("zeroed")
        setup = sem("setup")
        ring_filled = sem("ring_filled")
        ring_free = [sem(f"ring_free{b}") for b in range(3)]
        scored = sem("scored")
        var_done, rstd_done = sem("var_done"), sem("rstd_done")
        xn_done = sem("xn_done")
        max_done = sem("max_done")
        exp_done = sem("exp_done")
        any_filled = sem("any_filled")
        summed = sem("summed")
        on_done = sem("on_done")
        s2_sub, s2_exp, s2_mix = sem("s2_sub"), sem("s2_exp"), sem("s2_mix")
        diff_done, gate_exp = sem("diff_done"), sem("gate_exp")
        mixed = sem("mixed")
        lg_sub, lg_exp, gates_done = sem("lg_sub"), sem("lg_exp"), sem("gates_done")
        g_filled, u_filled = sem("g_filled"), sem("u_filled")
        silu_done = sem("silu_done")
        h_done = sem("h_done")
        y_done, y_copied = sem("y_done"), sem("y_copied")
        apart = sem("apart")
        dve_step = sem("dve_step")
        stored = sem("stored")
        out_free = sem("out_free")

        N_TILES = L0_TILES + L1_TILES
        N_LOADS = dict(w=8, mask=2, experts=7)

        def filled(g, name):
            return g * FILLS + AT[name] + 1

        def await_bank(eng, g, name):
            k = AT[name]
            eng.wait_ge(ring_free[k % 3], g * USES[k % 3] + k // 3 + 1)

        def await_copy(eng, g, name):
            k = AT[name]
            eng.wait_ge(ring_free[k % 3], g * USES[k % 3] + k // 3 + 2)

        def await_inner(eng, g, layer, t):
            if layer == 0 and t >= E:
                eng.wait_ge(h_done, g * (L0_TILES - E) + t - E + 1)
            else:
                await_copy(eng, g, f"g{'BD'[layer]}{t}")

        def emptied(name):
            return ring_free[AT[name] % 3]

        def real(tile):
            return tile.rearrange("p (n q) -> p n q", q=HALF)[:, :, 0:S]

        lo, hi, _ = interpolation()
        assert all(hi == lo + 1)
        PERIOD = next(r for r in range(1, S) if all(lo[i + r] - lo[i] == lo[r] - lo[0] for i in range(S - r)))
        STEP = int(lo[PERIOD] - lo[0])

        x_dram = d["x"].rearrange("(p h) s e -> h s p e", h=2)
        out_dram = d["out"].rearrange("(p h) s e -> h s p e", h=2)
        sel_dram = d["ctx"].rearrange("(p h) n e -> h n p e", h=2)
        rows_dram = d["ctx"].rearrange("(p h) (r j) e -> p r h (j e)", h=2, j=BLOCKS)
        cols_dram = d["ctxT"].rearrange("(p h) e n -> p e h n", h=2)

        block = ctx.enter_context(nc.Block())

        @block.sync
        def _(sp):
            def load_tokens(g):
                if not isinstance(g, int):
                    sp.wait_ge(x_taken, g)
                for half in range(2):
                    sp.dma_start(x_in[HALF * half:HALF * half + S, :, :],
                                 x_dram[half, :, bass.ds(g * PAIRS, PAIRS), :]).then_inc(x_loaded, 16)

            def load_selected(g):
                if not isinstance(g, int):
                    sp.wait_ge(ring_filled, filled(g - 1, "sel1"))
                for half in range(2):
                    for r in range(PERIOD):
                        n, first = len(range(r, S, PERIOD)), HALF * half + r
                        sp.dma_start(
                            sel[first:first + PERIOD * (n - 1) + 1:PERIOD, :, :, :].rearrange("q p w e -> q p (w e)"),
                            bass.AP(d["ctx"].tensor, (half * S2 + int(lo[r])) * D + g * PAIRS * 2 * S2 * D,
                                    [[STEP * D, n], [2 * S2 * D, PAIRS], [1, 2 * D]]),
                        ).then_inc(sel_loaded, 16)

            def load_context(g):
                for s in range(PAIRS):
                    if not isinstance(g, int):
                        sp.wait_ge(scored, (g - 1) * 2 * PAIRS + PAIRS + s + 1)
                    sp.dma_start(cols[:, s].rearrange("p h j r -> p h (j r)"),
                                 cols_dram[bass.ds(g * PAIRS + s, 1)].rearrange("a e h n -> (a e) h n")
                                 ).then_inc(cols_loaded[s], 16)
                    if not isinstance(g, int):
                        sp.wait_ge(summed, (g - 1) * 2 * PAIRS + PAIRS + s + 1)
                    src = rows_dram[bass.ds(g * PAIRS + s, 1)].rearrange("a r h n -> (a r) h n")
                    dst = rows[:, s].rearrange("p h j e -> p h (j e)")
                    sp.dma_start(dst[0:MAIN], src[0:MAIN]).then_inc(rows_loaded[s], 16)
                    sp.dma_start(dst[MAIN:BR], src[MAIN:BR]).then_inc(rows_loaded[s], 16)

            def store(g):
                await_copy(sp, g, "yD")
                for half in range(2):
                    sp.dma_start(out_dram[half, :, bass.ds(g * PAIRS, PAIRS), :],
                                 x_out[HALF * half:HALF * half + S, :, :]).then_inc(stored, 16)
                sp.wait_ge(stored, 32 * g + 32)
                sp.sem_inc(out_free, 1)

            sp.sem_inc(out_free, 1)
            sp.wait_ge(zeroed, N_ZEROED)
            load_tokens(0)
            load_selected(0)
            load_context(0)
            with sp.Fori(1, GROUPS) as g:
                load_tokens(g)
                load_selected(g)
                load_context(g)
                store(g - 1)
            store(GROUPS - 1)

        @block.gpsimd
        def _(pool):
            for tile, value in [(x_in[:, :, :], 0.0), (sel[:, :, :, :], 0.0), (minus_half[:, :], -0.5),
                                (p2[:, :, :], 0.0), (gates3[:, :, :], 0.0), (yT[:, :], 0.0), (ones[:, :], 1.0)]:
                pool.memset(tile, value).then_inc(zeroed, 1)
            pool.wait_ge(zeroed, N_ZEROED)

            def rstd_of(g, n):
                pool.wait_ge(var_done, g * NORMS + n + 1)
                pool.tensor_tensor(rstd[:, :], var[:, :], minus_half[:, :], ALU.pow).then_inc(rstd_done, 1)

            with pool.Fori(0, GROUPS) as g:
                rstd_of(g, 0)
                await_copy(pool, g, "s2c")
                await_copy(pool, g, "c2s")
                pool.tensor_tensor(diff[:, :], c2sT[:, :], s2cT[:, :], ALU.subtract).then_inc(diff_done, 1)
                for n in range(1, NORMS):
                    rstd_of(g, n)

        @block.tensor
        def _(pe):
            pe.wait_ge(w_in, 16 * N_LOADS["w"])
            pe.wait_ge(zeroed, N_ZEROED)
            pe.wait_ge(setup, N_SETUP - 1)
            pe.matmul(ps[:, 0, 0:HALF], ones[0:S, :], any_diag[0:S, :], start=True, stop=True).then_inc(any_filled, 1)
            pe.wait_ge(setup, N_SETUP)

            def transposes(g, name, tiles, identity, out):
                await_bank(pe, g, name)
                for k, t in enumerate(tiles):
                    mm = pe.transpose(out(k), t, identity)
                mm.then_inc(ring_filled, 1)

            def normed(g, name, n):
                pe.wait_ge(xn_done, g * NORMS + n + 1)
                transposes(g, name, [xn[:, s, :] for s in range(PAIRS)], W["ident"],
                           lambda k: ring(name)[:, k * 128:(k + 1) * 128])

            def project(g, name, weight, source, of):
                await_copy(pe, g, of)
                await_bank(pe, g, name)
                pe.matmul(ring(name), weight, source, start=True, stop=True).then_inc(ring_filled, 1)

            def pair_scores(g, s, layer):
                if layer == 0:
                    pe.wait_ge(cols_loaded[s], 16 * g + 16)
                for c in range(3):
                    for half in range(2):
                        mm = pe.matmul(ps[HALF * half:HALF * half + HALF, c, 0:CHUNK],
                                       qk[:, s * PAIR + HALF * half:s * PAIR + HALF * half + HALF],
                                       cols[:, s, half, 4 * c:4 * c + 4, :], start=True, stop=True)
                mm.then_inc(scored, 1)

            def turn_probs(g, s, layer):
                pe.wait_ge(exp_done, g * 2 * PAIRS + layer * PAIRS + s + 1)
                flat = prob[:, :, :].rearrange("p c n -> p (c n)")
                for c in range(3):
                    name = f"pt{'AC'[layer]}{s}.{c}"
                    transposes(g, name, [flat[:, (4 * c + k) * BR:(4 * c + k + 1) * BR] for k in range(4)],
                               W["ident"], lambda k: ring(name)[0:BR, k * 128:(k + 1) * 128])

            def context_sum(g, s, layer):
                if layer == 0:
                    pe.wait_ge(rows_loaded[s], 32 * g + 32)
                bank = ps[:, 6 + s % 2, 0:D]
                if s >= 2:
                    pe.wait_ge(on_done, g * 2 * PAIRS + layer * PAIRS + s - 1)
                for j in range(BLOCKS):
                    if j % 4 == 0:
                        await_copy(pe, g, f"pt{'AC'[layer]}{s}.{j // 4}")
                    for half in range(2):
                        mm = pe.matmul(bank[HALF * half:HALF * half + HALF, :],
                                       pT[0:BR, j, HALF * half:HALF * half + HALF],
                                       rows[0:BR, s, half, j, :], start=(j == 0), stop=(j == BLOCKS - 1))
                mm.then_inc(summed, 1)

            def experts(g, layer):
                tiles = [L0_TILES, L1_TILES][layer]
                routed = [E, L1_TILES][layer]
                up, down, spread = [(up0, down0, spread0), (up1, down1, spread1)][layer]
                tag = "BD"[layer]
                pe.wait_ge(experts_in, 16 * N_LOADS["experts"])

                def down_product(t):
                    M = min(128, up.shape[2] - 128 * t)
                    await_inner(pe, g, layer, t)
                    mm = pe.matmul(ps[:, Y_BANK, 0:GR], down[0:M, t, :], h[0:M, t % 2, :],
                                   start=(t == 0), stop=(t == tiles - 1))
                    if t == tiles - 1:
                        mm.then_inc(y_done, 1)

                for t in range(tiles):
                    M = min(128, up.shape[2] - 128 * t)
                    if t >= 2:
                        await_inner(pe, g, layer, t - 2)
                    pe.matmul(ps[0:M, G_BANKS[t % 2], 0:GR], up[:, 0, t * 128:t * 128 + M], real(xnT[:, :]),
                              start=True, stop=True).then_inc(g_filled, 1)
                    pe.matmul(ps[0:M, U_BANKS[t % 2], 0:GR], up[:, 1, t * 128:t * 128 + M], real(xnT[:, :]),
                              start=True, stop=True).then_inc(u_filled, 1)
                    if t < routed:
                        name = f"g{tag}{t}"
                        if t == 0:
                            await_copy(pe, g, f"gt{tag}")
                        await_bank(pe, g, name)
                        pe.matmul(ring(name)[0:M, 0:GR], spread[:, t, 0:M], real(gatesT[:, :]),
                                  start=True, stop=True).then_inc(ring_filled, 1)
                    if t >= 1:
                        down_product(t - 1)
                down_product(tiles - 1)
                name = f"y{tag}"
                pe.wait_ge(y_copied, g * 2 + layer + 1)
                transposes(g, name, [yT[:, s * 128:(s + 1) * 128] for s in range(PAIRS)], W["ident"],
                           lambda k: ring(name)[:, k * 128:(k + 1) * 128])

            def route(g, layer):
                tag = "BD"[layer]
                weight, n = [(router[:, 0:E], E), (router[:, E:2 * E + 1], E + 1)][layer]
                name = f"lg{tag}"
                await_copy(pe, g, f"xn{tag}")
                await_bank(pe, g, name)
                for s in range(PAIRS):
                    mm = pe.matmul(ring(name)[:, s * n:(s + 1) * n], xnT[:, s * 128:(s + 1) * 128], weight,
                                   start=True, stop=True)
                mm.then_inc(ring_filled, 1)
                name = f"gt{tag}"
                pe.wait_ge(gates_done, g * 2 + layer + 1)
                transposes(g, name, [gates3[:, s, :] for s in range(PAIRS)], identb[:, :],
                           lambda k: ring(name).bitcast(BF16)[0:GATE_ROWS, k * 128:(k + 1) * 128])

            with pe.Fori(0, GROUPS) as g:
                normed(g, "xnA", 0)
                project(g, "q", W["WqcT"], xnT[:, :], "xnA")
                project(g, "qk", W["Wks"], qT[:, :], "q")
                project(g, "kc", W["WkcT"], xnT[:, :], "xnA")
                await_bank(pe, g, "vc")
                for s in range(PAIRS):
                    mm = pe.matmul(ring("vc")[:, s * D:(s + 1) * D], xnT[:, s * 128:(s + 1) * 128], W["WvcT"],
                                   start=True, stop=True)
                mm.then_inc(ring_filled, 1)
                pe.wait_ge(sel_loaded, (g + 1) * 16 * 2 * PERIOD)
                for c in range(2):
                    name = f"sel{c}"
                    transposes(g, name, [sel[:, 2 * c + k // 2, k % 2, :] for k in range(4)], W["ident"],
                               lambda k: ring(name)[:, k * 128:(k + 1) * 128])
                for c in range(2):
                    project(g, f"qs{c}", W["WqsT"], selT[:, c * 512:(c + 1) * 512], f"sel{c}")
                await_copy(pe, g, "qk")
                for s in range(PAIRS):
                    pair_scores(g, s, 0)
                    if s == 0:
                        await_copy(pe, g, "kc")
                        for c in range(2):
                            name = f"s2{c}"
                            await_copy(pe, g, f"qs{c}")
                            await_bank(pe, g, name)
                            for k in range(4):
                                pair = 2 * c + k // 2
                                mm = pe.matmul(ring(name)[:, k * 128:(k + 1) * 128], qsT[:, 4 * c + k, :],
                                               kcT[:, pair * PAIR:(pair + 1) * PAIR], start=True, stop=True)
                            mm.then_inc(ring_filled, 1)
                    if s >= 1:
                        context_sum(g, s - 1, 0)
                    if s == 1:
                        pe.wait_ge(s2_mix, g + 1)
                        transposes(g, "p2", [p2[:, k, :] for k in range(PAIRS)], W["ident"],
                                   lambda k: ring("p2")[:, k * 128:(k + 1) * 128])
                    if s == 2:
                        await_copy(pe, g, "p2")
                        await_copy(pe, g, "vc")
                        await_bank(pe, g, "s2c")
                        for k in range(PAIRS):
                            mm = pe.matmul(ring("s2c")[:, k * 128:(k + 1) * 128], vc[:, k, :],
                                           p2T[:, k * 128:(k + 1) * 128], start=True, stop=True)
                        mm.then_inc(ring_filled, 1)
                    turn_probs(g, s, 0)
                context_sum(g, PAIRS - 1, 0)
                pe.wait_ge(on_done, g * 2 * PAIRS + PAIRS)
                transposes(g, "onA", [on[:, s, :] for s in range(PAIRS)], W["ident"],
                           lambda k: ring("onA")[:, k * 128:(k + 1) * 128])
                project(g, "c2s", W["WvsT"], onT[:, :], "onA")
                await_copy(pe, g, "s2c")
                await_copy(pe, g, "c2s")
                await_bank(pe, g, "gate")
                pe.matmul(ring("gate"), W["WgaT"], c2sT[:, :], start=True, stop=False)
                pe.matmul(ring("gate"), W["WgbT"], s2cT[:, :], start=False, stop=True).then_inc(ring_filled, 1)
                pe.wait_ge(mixed, g + 1)
                transposes(g, "dx", [gate[:, s * 128:(s + 1) * 128] for s in range(PAIRS)], W["ident"],
                           lambda k: ring("dx")[:, k * 128:(k + 1) * 128])
                normed(g, "xnB", 1)
                route(g, 0)
                experts(g, 0)
                normed(g, "xnC", 2)
                project(g, "q1", W["wi"], xnT[:, :], "xnC")
                project(g, "qw", W["wiT"], qT[:, :], "q1")
                await_copy(pe, g, "qw")
                for s in range(PAIRS):
                    pair_scores(g, s, 1)
                    if s >= 1:
                        context_sum(g, s - 1, 1)
                    turn_probs(g, s, 1)
                context_sum(g, PAIRS - 1, 1)
                pe.wait_ge(on_done, g * 2 * PAIRS + 2 * PAIRS)
                transposes(g, "onC", [on[:, s, :] for s in range(PAIRS)], W["ident"],
                           lambda k: ring("onC")[:, k * 128:(k + 1) * 128])
                await_copy(pe, g, "onC")
                await_bank(pe, g, "o1")
                for s in range(PAIRS):
                    bank = ring("o1")[:, s * D:(s + 1) * D]
                    pe.matmul(bank, xnT[:, s * 128:(s + 1) * 128], W["wi"], start=True, stop=False)
                    mm = pe.matmul(bank, onT[:, s * 128:(s + 1) * 128], W["wi"], start=False, stop=True)
                mm.then_inc(ring_filled, 1)
                normed(g, "xnD", 3)
                route(g, 1)
                experts(g, 1)

        @block.scalar
        def _(act):
            for dst, src in [
                (w[:, :, :], d["w"]), (bias[:, :], d["bias"]),
                (bv_c_row[:, :], d["bv_c"].partition_broadcast(128)),
                (gate_bias[:, :], d["gate_bias"].partition_broadcast(128)),
                (router[:, :], d["router"]),
                (identb[:, :], d["identb"]),
                (before[:, :, :].rearrange("p e j -> p (e j)"), d["before"].partition_broadcast(128)),
                (w_interp[:, :], d["w_interp"]),
            ]:
                act.dma_start(dst, src).then_inc(w_in, 16)
            for half in range(2):
                act.dma_start(mask_u8[HALF * half:HALF * half + S, :], d["mask"]).then_inc(mask_in, 16)
            for dst, src in [
                (up0[:, :, :], d["up0"]), (down0[:, :, :], d["down0"]), (spread0[:, :, :], d["spread0"]),
                (up1[:, :, :], d["up1"]), (down1[:, 0:L1_TILES - 1, :], d["down1"][:, 0:L1_TILES - 1, :]),
                (down1[0:L1_ROWS % 128, L1_TILES - 1, :], d["down1"][0:L1_ROWS % 128, L1_TILES - 1, :]),
                (spread1[:, :, :], d["spread1"]),
            ]:
                act.dma_start(dst, src).then_inc(experts_in, 16)
            act.wait_ge(w_in, 16 * N_LOADS["w"])
            act.wait_ge(setup, N_SETUP)
            act.wait_ge(zeroed, N_ZEROED)

            def copy(g, name, out, source=None, bias=None):
                act.wait_ge(ring_filled, filled(g, name))
                source = ring(name) if source is None else source
                if bias is None:
                    act.copy(out, source).then_inc(emptied(name), 1)
                else:
                    act.activation(out, source, ACT.Identity, bias=bias).then_inc(emptied(name), 1)

            def exps(g, s, layer):
                act.wait_ge(max_done, g * 2 * PAIRS + layer * PAIRS + s + 1)
                act.activation(prob[:, :, :], scores if layer == 0 else prob[:, :, :], ACT.Exp,
                               bias=ntop[:, s:s + 1], accum_out=total[:, s:s + 1]).then_inc(exp_done, 1)

            def probs(g, s, layer):
                name = f"pt{'AC'[layer]}{s}.1"
                copy(g, name, pT[0:BR, 4:8, :], ring(name)[0:BR, :])

            def route(g, layer):
                act.wait_ge(lg_sub, g * 2 + layer + 1)
                act.activation(lg[:, :, 0:E + layer], lg[:, :, 0:E + layer], ACT.Exp).then_inc(lg_exp, 1)

            def experts(g, layer):
                tiles = [L0_TILES, L1_TILES][layer]
                inner = [L0_TILES * 128, L1_ROWS][layer]
                for t in range(tiles):
                    M = min(128, inner - 128 * t)
                    act.wait_ge(g_filled, g * N_TILES + layer * L0_TILES + t + 1)
                    if t >= 2:
                        await_inner(act, g, layer, t - 2)
                    act.activation(sg[0:M, t % 2, :], ps[0:M, G_BANKS[t % 2], 0:GR], ACT.Silu).then_inc(silu_done, 1)
                act.wait_ge(y_done, g * 2 + layer + 1)
                act.copy(real(yT[:, :]), ps[:, Y_BANK, 0:GR].rearrange("p (n q) -> p n q", q=S)).then_inc(y_copied, 1)

            with act.Fori(0, GROUPS) as g:
                copy(g, "xnA", xnT[:, :])
                copy(g, "q", qT[:, :], bias=Bc["bq_c"])
                for c in range(2):
                    copy(g, f"sel{c}", selT[:, c * 512:(c + 1) * 512])
                for c in range(2):
                    copy(g, f"qs{c}", qsT[:, 4 * c:4 * c + 4, :].rearrange("p a b -> p (a b)"), bias=Bc["bq_s"])
                for s in range(PAIRS):
                    exps(g, s, 0)
                    if s == 0:
                        act.wait_ge(s2_sub, g + 1)
                        act.activation(s2[:, :, :], s2[:, :, :], ACT.Exp).then_inc(s2_exp, 1)
                    if s == 1:
                        copy(g, "p2", p2T[:, :])
                    if s == 2:
                        copy(g, "s2c", s2cT[:, :])
                    probs(g, s, 0)
                copy(g, "onA", onT[:, :])
                act.wait_ge(ring_filled, filled(g, "gate"))
                act.activation(gate[:, :], ring("gate"), ACT.Exp, bias=neg_bg[:, 0:1], scale=-1.0
                               ).then_inc(emptied("gate"), 1)
                copy(g, "xnB", xnT[:, :])
                route(g, 0)
                experts(g, 0)
                copy(g, "xnC", xnT[:, :])
                copy(g, "q1", qT[:, :])
                for s in range(PAIRS):
                    exps(g, s, 1)
                    probs(g, s, 1)
                copy(g, "onC", onT[:, :])
                copy(g, "xnD", xnT[:, :])
                route(g, 1)
                experts(g, 1)

        @block.vector
        def _(dve):
            def wait_apart(semaphore, value):
                dve.wait_ge(semaphore, value)
                dve.sem_inc(apart, 1)

            class Steps:
                def __init__(self, semaphore, count):
                    self.semaphore, self.count, self.g, self.n = semaphore, count, 0, 0

                def start(self, g):
                    self.g, self.n = g, 0

                def step(self, instruction):
                    instruction.then_inc(self.semaphore, 1)
                    self.n += 1
                    dve.wait_ge(self.semaphore, self.g * self.count + self.n)

                def step_apart(self, instruction):
                    instruction.then_inc(self.semaphore, 1)
                    self.n += 1
                    wait_apart(self.semaphore, self.g * self.count + self.n)

            own = Steps(dve_step, DVE_STEPS)
            first = Steps(setup, N_SETUP)

            first.step(dve.memset(penalty[:, :, :], 0.0))
            dve.wait_ge(w_in, 16 * N_LOADS["w"])
            first.step(dve.tensor_scalar(neg_bg[:, :], Bc["bg"], -1.0, None, ALU.mult))
            dve.wait_ge(mask_in, 16 * N_LOADS["mask"])
            for half in range(2):
                q = slice(HALF * half, HALF * half + S)
                first.step(dve.tensor_scalar(penalty[q, :, :].rearrange("p c (j r) -> p (c j) r", j=4),
                                             mask_u8[q, :].rearrange("p (r j) -> p j r", j=BLOCKS),
                                             -1.0, -MASKED, ALU.add, ALU.mult))
            first.step(dve.tensor_reduce(any_col[0:S, :], mask_u8[0:S, :], X, ALU.max))
            first.step(dve.tensor_scalar(any_diag[0:S, :], W["ident"][0:S, 0:HALF], any_col[0:S, 0:1], None, ALU.mult))
            dve.wait_ge(any_filled, 1)
            for b in range(3):
                dve.sem_inc(ring_free[b], 1)
            first.step(dve.tensor_copy(any_row[:, :], ps[:, 0, 0:HALF]))
            assert first.n == N_SETUP, first.n

            def norm(g, n):
                for s in range(PAIRS):
                    ins = dve.bn_stats(stats[:, s, :], x[:, s, :])
                own.step_apart(ins)
                for s in range(PAIRS):
                    ins = dve.bn_aggr(mv[:, s, :], stats[:, s, :])
                own.step(ins)
                dve.tensor_scalar(var[:, :], mv[:, :, 1], EPS, None, ALU.add).then_inc(var_done, 1)
                dve.wait_ge(rstd_done, g * NORMS + n + 1)
                for s in range(PAIRS):
                    ins = dve.tensor_scalar(xn[:, s, :], x[:, s, :], mv[:, s, 0:1], rstd[:, s:s + 1],
                                            ALU.subtract, ALU.mult)
                ins.then_inc(xn_done, 1)

            def wait_filled(g, name):
                dve.wait_ge(ring_filled, filled(g, name))

            def add_to_x(g, name):
                wait_filled(g, name)
                dve.tensor_tensor(x[:, :, :], x[:, :, :], ring(name).rearrange("p (s e) -> p s e", s=PAIRS),
                                  ALU.add).then_inc(emptied(name), 1)
                await_copy(dve, g, name)

            def probs(g, s, layer):
                for c in (0, 2):
                    name = f"pt{'AC'[layer]}{s}.{c}"
                    wait_filled(g, name)
                    dve.tensor_copy(pT[0:BR, 4 * c:4 * c + 4, :].rearrange("p a b -> p (a b)"), ring(name)[0:BR, :]
                                    ).then_inc(emptied(name), 1)

            def normalise(g, s, layer):
                n = g * 2 * PAIRS + layer * PAIRS + s + 1
                dve.wait_ge(exp_done, n)
                own.step(dve.reciprocal(rtotal[:, s:s + 1], total[:, s:s + 1]))
                dve.wait_ge(summed, n)
                dve.tensor_scalar(on[:, s, :], ps[:, 6 + s % 2, 0:D], rtotal[:, s:s + 1], None, ALU.mult
                                  ).then_inc(on_done, 1)

            def halves():
                return [slice(HALF * h, HALF * h + HALF) for h in range(2)]

            def small_softmax(g):
                for c in range(2):
                    name = f"s2{c}"
                    wait_filled(g, name)
                    blocks = ring(name).rearrange("p (k t) -> p k t", k=4)
                    for hs in halves():
                        ins = dve.tensor_copy(s2[hs, 4 * c:4 * c + 4, :], blocks[hs, :, hs.start:hs.start + S])
                    ins.then_inc(emptied(name), 1)
                await_copy(dve, g, "s20")
                await_copy(dve, g, "s21")
                own.step(dve.tensor_reduce(s2max[:, :], s2[:, :, :], X, ALU.max))
                dve.tensor_tensor(s2[:, :, :], s2[:, :, :],
                                  s2max[:, :].unsqueeze(2).to_broadcast([128, PAIRS * 2, S]),
                                  ALU.subtract).then_inc(s2_sub, 1)

            def small_mix(g):
                dve.wait_ge(s2_exp, g + 1)
                own.step(dve.tensor_reduce(s2sum[:, :], s2[:, :, :], X, ALU.add))
                own.step(dve.reciprocal(coef[:, :], s2sum[:, :]))
                own.step(dve.tensor_tensor(coef[:, :], coef[:, :], w_interp[:, :], ALU.mult))
                own.step(dve.tensor_tensor(s2[:, :, :], s2[:, :, :],
                                           coef[:, :].unsqueeze(2).to_broadcast([128, PAIRS * 2, S]), ALU.mult))
                both = s2[:, :, :].rearrange("p (s w) k -> p s w k", w=2)
                for hs in halves():
                    ins = dve.tensor_tensor(p2[hs, :, hs.start:hs.start + S], both[hs, :, 0, :], both[hs, :, 1, :],
                                            ALU.add)
                ins.then_inc(s2_mix, 1)

            def route(g, layer):
                tag = "BD"[layer]
                n = E + layer
                name = f"lg{tag}"
                wait_filled(g, name)
                z = ring(name)[:, 0:PAIRS * n].rearrange("p (s e) -> p s e", s=PAIRS)
                own.step(dve.tensor_reduce(lmax[:, :], z[:, :, 0:E], X, ALU.max))
                if layer:
                    dve.tensor_scalar(lg[:, :, E:E + 1], z[:, :, E:E + 1], -1.0, None, ALU.mult)
                dve.tensor_tensor(lg[:, :, 0:E], z[:, :, 0:E], lmax[:, :].unsqueeze(2).to_broadcast([128, PAIRS, E]),
                                  ALU.subtract).then_inc(emptied(name), 1)
                await_copy(dve, g, name)
                dve.sem_inc(lg_sub, 1)
                dve.wait_ge(lg_exp, g * 2 + layer + 1)
                score = lg[:, :, 0:E]
                own.step(dve.tensor_reduce(lsum[:, :], score, X, ALU.add))
                own.step(dve.reciprocal(lsum[:, :], lsum[:, :]))
                own.step(dve.tensor_tensor(score, score, lsum[:, :].unsqueeze(2).to_broadcast([128, PAIRS, E]),
                                           ALU.mult))
                if layer == 0:
                    own.step(dve.tensor_tensor(key[:, :, :], score,
                                               gate_bias[:, :].unsqueeze(1).to_broadcast([128, PAIRS, E]), ALU.add))
                    k = key[:, :, :]
                else:
                    own.step(dve.tensor_scalar(gates[:, :, E:E + 1], lg[:, :, E:E + 1], 1.0, None, ALU.add))
                    own.step(dve.reciprocal(gates[:, :, E:E + 1], gates[:, :, E:E + 1]))
                    k = score
                shape = [128, PAIRS, E, E]
                mine, other = k.unsqueeze(3).to_broadcast(shape), k.unsqueeze(2).to_broadcast(shape)
                dve.tensor_tensor(above[:, :, :, :], other, mine, ALU.is_gt)
                own.step(dve.tensor_tensor(tied[:, :, :, :], other, mine, ALU.is_equal))
                own.step(dve.tensor_tensor(tied[:, :, :, :], tied[:, :, :, :],
                                           before[:, :, :].unsqueeze(1).to_broadcast(shape), ALU.mult))
                own.step(dve.tensor_tensor(above[:, :, :, :], above[:, :, :, :], tied[:, :, :, :], ALU.add))
                own.step(dve.tensor_reduce(rank[:, :, :], above[:, :, :, :], X, ALU.add))
                own.step(dve.scalar_tensor_tensor(out=gates[:, :, 0:E], in0=rank[:, :, :], scalar=2.0, in1=score,
                                                  op0=ALU.is_lt, op1=ALU.mult))
                left = gates[:, :, 0:n]
                for part in range(3):
                    cut = gates3[:, :, 32 * part:32 * part + n]
                    ins = dve.tensor_copy(cut, left)
                    if part < 2:
                        own.step(ins)
                        own.step(dve.tensor_tensor(rest[:, :, 0:n], left, cut, ALU.subtract))
                        left = rest[:, :, 0:n]
                ins.then_inc(gates_done, 1)
                name = f"gt{tag}"
                wait_filled(g, name)
                dve.tensor_copy(gatesT[:, :], ring(name).bitcast(BF16)[0:GATE_ROWS, 0:GT]).then_inc(emptied(name), 1)

            def experts(g, layer):
                tiles = [L0_TILES, L1_TILES][layer]
                inner = [L0_TILES * 128, L1_ROWS][layer]
                for t in range(tiles):
                    M = min(128, inner - 128 * t)
                    n = g * N_TILES + layer * L0_TILES + t + 1
                    routed = layer == 1 or t < E
                    out = (hu if routed else h)[0:M, t % 2, :]
                    dve.wait_ge(u_filled, n)
                    dve.wait_ge(silu_done, n)
                    if t >= 2 and not routed:
                        dve.wait_ge(g_filled, n)
                    ins = dve.tensor_tensor(out, sg[0:M, t % 2, :], ps[0:M, U_BANKS[t % 2], 0:GR], ALU.mult)
                    if routed:
                        own.step(ins)
                        name = f"g{tag_of(layer)}{t}"
                        wait_filled(g, name)
                        dve.tensor_tensor(h[0:M, t % 2, :], out, ring(name)[0:M, 0:GR], ALU.mult
                                          ).then_inc(emptied(name), 1)
                    else:
                        ins.then_inc(h_done, 1)

            def tag_of(layer):
                return "BD"[layer]

            with dve.Fori(0, GROUPS) as g:
                own.start(g)
                dve.wait_ge(x_loaded, 32 * g + 32)
                dve.tensor_copy(x[:, :, :], x_in[:, :, :]).then_inc(x_taken, 1)
                dve.wait_ge(x_taken, g + 1)
                norm(g, 0)
                wait_filled(g, "qk")
                dve.tensor_scalar(qk[:, :], ring("qk"), SCALE, None, ALU.mult).then_inc(emptied("qk"), 1)
                wait_filled(g, "kc")
                dve.tensor_scalar(kcT[:, :], ring("kc"), Bc["bk_c"], SCALE, ALU.add, ALU.mult
                                  ).then_inc(emptied("kc"), 1)
                wait_filled(g, "vc")
                dve.tensor_tensor(vc[:, :, :], ring("vc").rearrange("p (s e) -> p s e", s=PAIRS),
                                  bv_c_row[:, :].unsqueeze(1).to_broadcast([128, PAIRS, D]), ALU.add
                                  ).then_inc(emptied("vc"), 1)
                for s in range(PAIRS):
                    dve.wait_ge(scored, g * 2 * PAIRS + s + 1)
                    dve.tensor_reduce(ntop[:, s:s + 1], scores, mybir.AxisListType.XY, ALU.max, negate=True
                                      ).then_inc(max_done, 1)
                    if s == 0:
                        small_softmax(g)
                    else:
                        normalise(g, s - 1, 0)
                    probs(g, s, 0)
                    if s == 0:
                        small_mix(g)
                normalise(g, PAIRS - 1, 0)
                wait_filled(g, "c2s")
                dve.tensor_scalar(c2sT[:, :], ring("c2s"), Bc["bv_s"], None, ALU.add).then_inc(emptied("c2s"), 1)
                await_copy(dve, g, "gate")
                own.step(dve.tensor_scalar(gate[:, :], gate[:, :], 1.0, None, ALU.add))
                own.step(dve.reciprocal(gate[:, :], gate[:, :]))
                dve.wait_ge(diff_done, g + 1)
                own.step(dve.tensor_tensor(gate[:, :], gate[:, :], diff[:, :], ALU.mult))
                dve.tensor_tensor(gate[:, :], gate[:, :], s2cT[:, :], ALU.add).then_inc(mixed, 1)
                add_to_x(g, "dx")
                norm(g, 1)
                route(g, 0)
                experts(g, 0)
                add_to_x(g, "yB")
                norm(g, 2)
                wait_filled(g, "qw")
                dve.scalar_tensor_tensor(out=qk[:, :].rearrange("p (n q) -> p n q", q=HALF),
                                         in0=ring("qw").rearrange("p (n q) -> p n q", q=HALF), scalar=SCALE,
                                         in1=any_row[:, :].unsqueeze(1).to_broadcast([128, 2 * PAIRS, HALF]),
                                         op0=ALU.mult, op1=ALU.mult).then_inc(emptied("qw"), 1)
                for s in range(PAIRS):
                    wait_apart(scored, g * 2 * PAIRS + PAIRS + s + 1)
                    own.step(dve.tensor_tensor_reduce(prob[:, :, :], scores, penalty[:, :, :], 1.0, LOWEST,
                                                      ALU.add, ALU.max, top[:, s:s + 1]))
                    dve.tensor_scalar(ntop[:, s:s + 1], top[:, s:s + 1], -1.0, None, ALU.mult).then_inc(max_done, 1)
                    if s >= 1:
                        normalise(g, s - 1, 1)
                    probs(g, s, 1)
                normalise(g, PAIRS - 1, 1)
                add_to_x(g, "o1")
                norm(g, 3)
                route(g, 1)
                experts(g, 1)
                wait_filled(g, "yD")
                dve.wait_ge(out_free, g + 1)
                dve.tensor_tensor(x_out[:, :, :], x[:, :, :], ring("yD").rearrange("p (s e) -> p s e", s=PAIRS),
                                  ALU.add).then_inc(emptied("yD"), 1)
                await_copy(dve, g, "yD")
                assert own.n == DVE_STEPS, own.n


def kernel(**inputs):
    import ml_dtypes
    import numpy as np
    import concourse.bacc as bacc
    from concourse.bass_utils import run_bass_kernel_spmd

    a = {k: np.asarray(v) for k, v in inputs.items()}
    f32 = np.float32

    def T(name):
        return a[name].T

    def side(*blocks):
        return np.concatenate(blocks, axis=1)

    def tiles(m):
        m = np.concatenate([m, np.zeros((-len(m) % 128, m.shape[1]), m.dtype)], axis=0)
        return m.reshape(-1, 128, m.shape[1]).transpose(1, 0, 2)

    _, _, w_hi = interpolation()
    w_interp = np.zeros((128, PAIRS, 2), f32)
    for half in range(2):
        w_interp[HALF * half:HALF * half + S, :, 0] = (f32(1) - w_hi)[:, None]
        w_interp[HALF * half:HALF * half + S, :, 1] = w_hi[:, None]

    def spread(rows_of_gate, n_tiles):
        m = np.zeros((GATE_ROWS, n_tiles, 128), ml_dtypes.bfloat16)
        for r, gate in enumerate(rows_of_gate):
            for part in range(3):
                m[32 * part + gate, r // 128, r % 128] = 1
        return m

    Wg = a["L0_xattn_Wg"]
    attention = {
        "WqcT": T("L0_xattn_Wq_c"), "Wks": a["L0_xattn_Wk_s"], "WvsT": T("L0_xattn_Wv_s"),
        "WqsT": T("L0_xattn_Wq_s"), "WkcT": T("L0_xattn_Wk_c"), "WvcT": T("L0_xattn_Wv_c"),
        "WgaT": Wg[:, :D].T, "WgbT": Wg[:, D:].T, "wi": a["L1_xattn_wi"], "wiT": T("L1_xattn_wi"),
        "ident": np.eye(128, dtype=f32),
    }
    w1, w3, w2 = a["L0_ffn_w1"], a["L0_ffn_w3"], a["L0_ffn_w2"]
    gu, dn = a["L1_ffn_experts_gate_up"], a["L1_ffn_experts_down"]
    arrays = {
        "x": a["x"], "ctx": a["ctx_1024"],
        "ctxT": a["ctx_1024"].reshape(BATCH, BR, BLOCKS, D).transpose(0, 3, 2, 1).reshape(BATCH, D, S2),
        "mask": a["mask_1xSxS2_bk0"][0],
        "w": np.stack([attention[n] for n in W_NAMES], axis=1),
        "bias": np.stack([a["L0_xattn_" + n] for n in B_NAMES], axis=1),
        "bv_c": a["L0_xattn_bv_c"], "gate_bias": a["L0_ffn_gate_bias"],
        "router": side(T("L0_ffn_gate_w"), T("L1_ffn_gate_w"), T("L1_ffn_shared_expert_gate_w")),
        "identb": np.eye(128, dtype=ml_dtypes.bfloat16),
        "before": np.tril(np.ones((E, E), f32), -1).reshape(-1),
        "w_interp": w_interp.reshape(128, -1),
        "up0": np.stack([side(*[m.T for m in w1], T("L0_ffn_sw1")), side(*[m.T for m in w3], T("L0_ffn_sw3"))], axis=1),
        "down0": tiles(np.concatenate([*[m.T for m in w2], T("L0_ffn_sw2")], axis=0)),
        "spread0": spread(np.arange(E * 128) // 128, E),
        "up1": np.stack([side(*[m[:I1].T for m in gu], T("L1_ffn_shared_gate_w")),
                         side(*[m[I1:].T for m in gu], T("L1_ffn_shared_up_w"))], axis=1),
        "down1": tiles(np.concatenate([*[m.T for m in dn], T("L1_ffn_shared_down_w")], axis=0)),
        "spread1": spread(np.minimum(np.arange(L1_ROWS) // I1, E), L1_TILES),
    }
    nc = bacc.Bacc("TRN2", target_bir_lowering=False, num_devices=1)
    given, dram = {}, {}
    for name, array in arrays.items():
        given["in_" + name] = np.ascontiguousarray(array)
        dram[name] = nc.dram_tensor("in_" + name, array.shape, mybir.dt.from_np(array.dtype), kind="ExternalInput").ap()
    dram["out"] = nc.dram_tensor("out_0", (BATCH, S, D), F32, kind="ExternalOutput").ap()
    build(nc, dram)
    return run_bass_kernel_spmd(nc, [given], core_ids=[0]).results[0]["out_0"]
```

```python
from contextlib import ExitStack

import concourse.bass as bass
from concourse import mybir

F32 = mybir.dt.float32
BF16 = mybir.dt.bfloat16
U8 = mybir.dt.uint8
ALU = mybir.AluOpType
ACT = mybir.ActivationFunctionType
X = mybir.AxisListType.X

BATCH, S, D, S2 = 32, 56, 128, 1500
HALF = 64
PAIR = 2 * HALF
PAIRS = 4
GROUPS = BATCH // (2 * PAIRS)
GT = PAIRS * PAIR
PARTS = 2
PP = PAIRS // PARTS
PT = PP * PAIR
PR = PP * 2 * S
BLOCKS = 12
BR = S2 // BLOCKS
MAIN = 112
BANK = 512
CHUNK = S2 // 3
E = 8
EPS = 1e-5
EULER = 2.718281828459045
SCALE = float(D) ** -0.5
MASKED = -1e10
LOWEST = -3.0e38

L0_TILES = E + 2
I1, SI1 = 176, 352
L1_ROWS = E * I1 + SI1
L1_TILES = -(-L1_ROWS // 128)
GATE_ROWS = 96

W_NAMES = ["WqcT", "Wks", "WvsT", "WqsT", "WkcT", "WvcT", "WgaT", "WgbT", "wi", "wiT", "ident"]
B_NAMES = ["bq_c", "bk_c", "bq_s", "bv_s", "bg", "bk_s"]

RING = [3, 4, 5]
SUM_BANKS = [6, 7]
DEPTH = 3
LAG = 2


STEPS = """
    take sel:0 stats:0,0 sel:1 qs:0 stats:0,1 norm:0,0 qs:1 xnT:0,0 norm:0,1 q:0 kc:0 xnT:0,1 qk:0 q:1 kc:1
    scores:0,0 vc:0 s2:0 s2exp:0 qk:1 turn:0,0 s2mix:0 scores:0,1 s2:1 s2exp:1 sum:0,0 turn:0,1 scores:0,2
    sum:0,1 p2:0 on:0,0 s2c:0 c2s:0 s2mix:1 turn:0,2 gate:0 mix:0 scores:0,3 p2:1 dx:0 stats:1,0 sum:0,2
    norm:1,0 turn:0,3 xnT:1,0 vc:1 lg:0,0 sum:0,3 softmax:0,0 tile:0,0,8 on:0,1 s2c:1 rank:0,0 c2s:1
    tile:0,0,9 gate:1 down:0,0,8 down:0,0,9 gates:0,0 mix:1 gt:0,0 dx:1 stats:1,1 tile:0,0,0 tile:0,0,1
    norm:1,1 tile:0,0,2 down:0,0,0 tile:0,0,3 xnT:1,1 down:0,0,1 down:0,0,2 lg:0,1 tile:0,0,4 down:0,0,3
    tile:0,0,5 tile:0,0,6 down:0,0,4 down:0,0,5 softmax:0,1 rank:0,1 tile:0,0,7 down:0,0,6 tile:0,1,8
    tile:0,1,9 down:0,0,7 y:0,0 gates:0,1 yT:0,0 down:0,1,8 down:0,1,9 gt:0,1 tile:0,1,0 tile:0,1,1 stats:2,0
    tile:0,1,2 norm:2,0 down:0,1,0 down:0,1,1 tile:0,1,3 tile:0,1,4 down:0,1,2 xnT:2,0 tile:0,1,5 down:0,1,3
    down:0,1,4 q1:0 tile:0,1,6 tile:0,1,7 qw:0 down:0,1,5 down:0,1,6 down:0,1,7 y:0,1 scores:1,0 yT:0,1
    stats:2,1 norm:2,1 turn:1,0 xnT:2,1 scores:1,1 q1:1 sum:1,0 qw:1 turn:1,1 scores:1,2 sum:1,1 on:1,0
    turn:1,2 o1:0 stats:3,0 scores:1,3 norm:3,0 sum:1,2 xnT:3,0 lg:1,0 turn:1,3 softmax:1,0 sum:1,3 rank:1,0
    gates:1,0 on:1,1 o1:1 gt:1,0 stats:3,1 tile:1,0,0 tile:1,0,1 norm:3,1 tile:1,0,2 down:1,0,0 tile:1,0,3
    xnT:3,1 down:1,0,1 down:1,0,2 lg:1,1 tile:1,0,4 down:1,0,3 tile:1,0,5 tile:1,0,6 down:1,0,4 down:1,0,5
    softmax:1,1 tile:1,0,7 tile:1,0,8 rank:1,1 down:1,0,6 tile:1,0,9 down:1,0,7 tile:1,0,10 gates:1,1
    down:1,0,8 tile:1,0,11 down:1,0,9 down:1,0,10 tile:1,0,12 gt:1,1 tile:1,0,13 down:1,0,11 tile:1,1,0
    down:1,0,12 tile:1,1,1 down:1,0,13 down:1,1,0 tile:1,1,2 down:1,1,1 tile:1,1,3 tile:1,1,4 down:1,1,2
    tile:1,1,5 down:1,1,3 down:1,1,4 tile:1,1,6 tile:1,1,7 down:1,1,5 down:1,1,6 tile:1,1,8 down:1,1,7
    tile:1,1,9 down:1,1,8 tile:1,1,10 tile:1,1,11 down:1,1,9 down:1,1,10 y:1,0 tile:1,1,12 tile:1,1,13
    down:1,1,11 yT:1,0 down:1,1,12 down:1,1,13 y:1,1 yT:1,1
"""
SCHEDULE = [(kind, *(map(int, at.split(",")) if at else ())) for kind, _, at in (word.partition(":") for word in STEPS.split())]


def routed(layer, t):
    return layer == 1 or t < E


def fills_of(kind, *at):
    if kind in ("sel", "qs", "q", "kc", "qk", "vc", "s2", "p2", "s2c", "c2s", "gate", "dx", "q1", "qw", "o1"):
        return [f"{kind}{at[0]}"]
    if kind in ("xnT", "on", "lg", "gt", "yT"):
        return [f"{kind}{at[0]}{at[1]}"]
    if kind == "turn":
        return [f"turn{at[0]}{at[1]}.{c}" for c in range(3)]
    if kind == "tile" and routed(at[0], at[2]):
        return [f"g{at[0]}{at[1]}.{at[2]}"]
    return []


NTH = {step: sum(other[0] == step[0] for other in SCHEDULE[:k]) + 1 for k, step in enumerate(SCHEDULE)}
PER = {kind: sum(step[0] == kind for step in SCHEDULE) for kind in {step[0] for step in SCHEDULE}}
assert len(NTH) == len(SCHEDULE)
ORDER = [name for step in SCHEDULE for name in fills_of(*step)]
AT = {name: k for k, name in enumerate(ORDER)}
FILLS = len(ORDER)
USES = [len(range(b, FILLS, 3)) for b in range(3)]
TILES = [step[1:] for step in SCHEDULE if step[0] == "tile"]
UNROUTED = [tile for tile in TILES if not routed(tile[0], tile[2])]
LAST_DOWN = {step[1:3]: step for step in SCHEDULE if step[0] == "down"}
FIRST_DOWN = {step[1:3]: step for step in reversed(SCHEDULE) if step[0] == "down"}
N_ZEROED = 8
N_SETUP = 7
DVE_STEPS = 142


def due(g, *step):
    return g * PER[step[0]] + NTH[step]


def in_flight(layer, part, t):
    return TILES.index((layer, part, t)) % DEPTH


def tile_rows(layer, t):
    return min(128, [L0_TILES * 128, L1_ROWS][layer] - 128 * t)


def interpolation():
    import numpy as np
    one = np.float32
    pos = (np.arange(S, dtype=one) + one(0.5)) * one(S2 / S) - one(0.5)
    pos = np.clip(pos, one(0), one(S2 - 1)).astype(one)
    lo = np.floor(pos).astype(np.int32)
    hi = np.minimum(lo + 1, S2 - 1)
    return lo, hi, (pos - lo.astype(one)).astype(one)


def build(nc, d):
    with ExitStack() as ctx:
        def sb(name, shape, dt=F32):
            return ctx.enter_context(nc.sbuf_tensor(name, shape, dt))

        def sem(name):
            return ctx.enter_context(nc.semaphore(name))

        w = sb("w", [128, len(W_NAMES), D])
        W = {n: w[:, i, :] for i, n in enumerate(W_NAMES)}
        bias = sb("bias", [128, len(B_NAMES)])
        Bc = {n: bias[:, i:i + 1] for i, n in enumerate(B_NAMES)}
        half_bg = sb("half_bg", [128, 1])
        bv_c_row = sb("bv_c_row", [128, D])
        gate_bias = sb("gate_bias", [128, E])
        router = sb("router", [128, 2 * E + 1])
        up0 = sb("up0", [128, 2, L0_TILES * 128])
        down0 = sb("down0", [128, L0_TILES, D])
        up1 = sb("up1", [128, 2, L1_ROWS])
        down1 = sb("down1", [128, L1_TILES, D])
        spread0 = sb("spread0", [GATE_ROWS, E, 128], BF16)
        spread1 = sb("spread1", [GATE_ROWS, L1_TILES, 128], BF16)
        identb = sb("identb", [128, 128], BF16)
        least_lead = sb("least_lead", [128, E, E])
        w_interp = sb("w_interp", [128, PAIRS * 2])
        penalty = sb("penalty", [128, 3, CHUNK])
        any_col = sb("any_col", [128, 1])
        any_diag = sb("any_diag", [HALF, HALF])
        ones = sb("ones", [HALF, 128])
        any_row = sb("any_row", [128, HALF])
        minus_half = sb("minus_half", [128, PAIRS])
        euler = sb("euler", [128, PP, E + 1])

        rows = sb("rows", [128, PAIRS, 2, BLOCKS, D])
        cols = sb("cols", [128, PAIRS, 2, BLOCKS, BR])
        sel = sb("sel", [128, PAIRS, 2, D])
        x_in = sb("x_in", [128, PAIRS, D])
        x = sb("x", [128, PAIRS, D])
        x_out = sb("x_out", [128, PAIRS, D])
        stats = sb("stats", [128, PAIRS, 6])
        mv = sb("mv", [128, PAIRS, 2])
        var = sb("var", [128, PAIRS])
        rstd = sb("rstd", [128, PAIRS])
        xn = sb("xn", [128, PAIRS, D])
        xnT = sb("xnT", [128, GT])
        qT = sb("qT", [128, GT])
        qk = sb("qk", [128, GT])
        kcT = sb("kcT", [128, GT])
        vc = sb("vc", [128, PAIRS, D])
        late = sb("late", [128, 4, GT])
        selT = late[:, 0:2, :].rearrange("p a b -> p (a b)")
        qsT = late[:, 2:4, :].rearrange("p a (k t) -> p (a k) t", k=4)
        onT, c2sT, gate, diff = (late[:, i, :] for i in range(4))
        lead = [late[:, 1, p * PT:p * PT + PP * E * E].rearrange("p (s e j) -> p s e j", s=PP, e=E)
                for p in range(PARTS)]
        mask_u8 = late[:, 3, :].bitcast(U8)[:, 0:S2]
        s2 = sb("s2", [128, PAIRS * 2, S])
        s2max = sb("s2max", [128, PAIRS * 2])
        s2sum = sb("s2sum", [128, PAIRS * 2])
        coef = sb("coef", [128, PAIRS * 2])
        p2 = sb("p2", [128, PAIRS, PAIR])
        p2T = sb("p2T", [128, GT])
        s2cT = sb("s2cT", [128, GT])
        top = sb("top", [128, PAIRS])
        ntop = sb("ntop", [128, PAIRS])
        minus_qb = sb("minus_qb", [128, PAIRS])
        total = sb("total", [128, PAIRS])
        rtotal = sb("rtotal", [128, PAIRS])
        work = sb("work", [128, S2 + BLOCKS * PAIR])
        prob = work[:, 0:S2].rearrange("p (c n) -> p c n", c=3)
        pT = work[:, S2:S2 + BLOCKS * PAIR].rearrange("p (j t) -> p j t", j=BLOCKS)
        sg, hu, h = (work[:, at:at + DEPTH * PR].rearrange("p (k t) -> p k t", k=DEPTH)
                     for at in (0, DEPTH * PR, S2))
        assert 2 * DEPTH * PR <= S2
        on = sb("on", [128, PAIRS, D])
        lg = sb("lg", [128, PAIRS, E + 1])
        lmax = sb("lmax", [128, PAIRS])
        lsum = sb("lsum", [128, PAIRS])
        key = sb("key", [128, PAIRS, E])
        rank = sb("rank", [128, PAIRS, E])
        gates = sb("gates", [128, PAIRS, E + 1])
        rest = sb("rest", [128, PAIRS, E + 1])
        gates3 = sb("gates3", [128, PAIRS, GATE_ROWS], BF16)
        gatesT = sb("gatesT", [GATE_ROWS, GT], BF16)
        yT = sb("yT", [128, GT])

        ps = ctx.enter_context(nc.psum_tensor("ps", [128, 8, BANK], F32))

        def ring(name):
            return ps[:, RING[AT[name] % 3], :]

        scores = ps[:, 0:3, 0:CHUNK]

        w_in = sem("w_in")
        mask_in = sem("mask_in")
        experts_in = sem("experts_in")
        x_loaded, x_taken = sem("x_loaded"), sem("x_taken")
        sel_loaded = sem("sel_loaded")
        rows_loaded = [sem(f"rows_loaded{s}") for s in range(PAIRS)]
        cols_loaded = [sem(f"cols_loaded{s}") for s in range(PAIRS)]
        zeroed = sem("zeroed")
        setup = sem("setup")
        any_filled = sem("any_filled")
        ring_filled = sem("ring_filled")
        ring_free = [sem(f"ring_free{b}") for b in range(3)]
        scored = sem("scored")
        max_done = sem("max_done")
        exp_done = sem("exp_done")
        summed = sem("summed")
        on_done = sem("on_done")
        var_done, rstd_done = sem("var_done"), sem("rstd_done")
        xn_done = sem("xn_done")
        s2_sub, s2_exp, s2_mix = sem("s2_sub"), sem("s2_exp"), sem("s2_mix")
        diff_done = sem("diff_done")
        mixed = sem("mixed")
        lg_sub, lg_exp = sem("lg_sub"), sem("lg_exp")
        gates_done = sem("gates_done")
        gu_filled = sem("gu_filled")
        silu_done = sem("silu_done")
        h_done = sem("h_done")
        y_done, y_copied = sem("y_done"), sem("y_copied")
        apart = sem("apart")
        dve_step = sem("dve_step")
        stored = sem("stored")
        out_free = sem("out_free")

        N_LOADS = dict(w=8, mask=2, experts=7)

        def filled(g, name):
            return g * FILLS + AT[name] + 1

        def await_bank(eng, g, name):
            k = AT[name]
            eng.wait_ge(ring_free[k % 3], g * USES[k % 3] + k // 3 + 1)

        def await_copy(eng, g, name):
            k = AT[name]
            eng.wait_ge(ring_free[k % 3], g * USES[k % 3] + k // 3 + 2)

        def await_ring(eng, g, fill, copied):
            k = AT[fill]
            counts = {k % 3: k // 3 + 1}
            for name in copied:
                k = AT[name]
                counts[k % 3] = max(counts.get(k % 3, 0), k // 3 + 2)
            for bank, count in sorted(counts.items()):
                eng.wait_ge(ring_free[bank], g * USES[bank] + count)

        def await_inner(eng, g, layer, part, t):
            if routed(layer, t):
                await_copy(eng, g, f"g{layer}{part}.{t}")
            else:
                eng.wait_ge(h_done, g * len(UNROUTED) + UNROUTED.index((layer, part, t)) + 1)

        def emptied(name):
            return ring_free[AT[name] % 3]

        def part_of(tile, p):
            return tile[:, p * PT:(p + 1) * PT]

        def real(tile):
            return tile.rearrange("p (n q) -> p n q", q=HALF)[:, :, 0:S]

        def pairs(p):
            return range(p * PP, (p + 1) * PP)

        def pslice(p):
            return slice(p * PP, (p + 1) * PP)

        lo, hi, _ = interpolation()
        assert all(hi == lo + 1)
        PERIOD = next(r for r in range(1, S) if all(lo[i + r] - lo[i] == lo[r] - lo[0] for i in range(S - r)))
        STEP = int(lo[PERIOD] - lo[0])

        x_dram = d["x"].rearrange("(p h) s e -> h s p e", h=2)
        out_dram = d["out"].rearrange("(p h) s e -> h s p e", h=2)
        sel_dram = d["ctx"].rearrange("(p h) n e -> h n p e", h=2)
        rows_dram = d["ctx"].rearrange("(p h) (r j) e -> p r h (j e)", h=2, j=BLOCKS)
        cols_dram = d["ctxT"].rearrange("(p h) e n -> p e h n", h=2)

        block = ctx.enter_context(nc.Block())

        @block.sync
        def _(sp):
            def load_tokens(g):
                if not isinstance(g, int):
                    sp.wait_ge(x_taken, g)
                for half in range(2):
                    sp.dma_start(x_in[HALF * half:HALF * half + S, :, :],
                                 x_dram[half, :, bass.ds(g * PAIRS, PAIRS), :]).then_inc(x_loaded, 16)

            def load_selected(g):
                if not isinstance(g, int):
                    sp.wait_ge(ring_filled, filled(g - 1, "sel1"))
                for half in range(2):
                    for r in range(PERIOD):
                        n, first = len(range(r, S, PERIOD)), HALF * half + r
                        sp.dma_start(
                            sel[first:first + PERIOD * (n - 1) + 1:PERIOD, :, :, :].rearrange("q p w e -> q p (w e)"),
                            bass.AP(d["ctx"].tensor, (half * S2 + int(lo[r])) * D + g * PAIRS * 2 * S2 * D,
                                    [[STEP * D, n], [2 * S2 * D, PAIRS], [1, 2 * D]]),
                        ).then_inc(sel_loaded, 16)

            def load_context(g):
                for s in range(PAIRS):
                    if not isinstance(g, int):
                        sp.wait_ge(scored, due(g - 1, "scores", 1, s))
                    sp.dma_start(cols[:, s].rearrange("p h j r -> p h (j r)"),
                                 cols_dram[bass.ds(g * PAIRS + s, 1)].rearrange("a e h n -> (a e) h n")
                                 ).then_inc(cols_loaded[s], 16)
                    if not isinstance(g, int):
                        sp.wait_ge(summed, due(g - 1, "sum", 1, s))
                    src = rows_dram[bass.ds(g * PAIRS + s, 1)].rearrange("a r h n -> (a r) h n")
                    dst = rows[:, s].rearrange("p h j e -> p h (j e)")
                    sp.dma_start(dst[0:MAIN], src[0:MAIN]).then_inc(rows_loaded[s], 16)
                    sp.dma_start(dst[MAIN:BR], src[MAIN:BR]).then_inc(rows_loaded[s], 16)

            def store(g):
                await_copy(sp, g, "yT11")
                for half in range(2):
                    sp.dma_start(out_dram[half, :, bass.ds(g * PAIRS, PAIRS), :],
                                 x_out[HALF * half:HALF * half + S, :, :]).then_inc(stored, 16)
                sp.wait_ge(stored, 32 * g + 32)
                sp.sem_inc(out_free, 1)

            sp.sem_inc(out_free, 1)
            sp.wait_ge(zeroed, N_ZEROED)
            load_tokens(0)
            load_selected(0)
            load_context(0)
            with sp.Fori(1, GROUPS) as g:
                load_tokens(g)
                load_selected(g)
                load_context(g)
                store(g - 1)
            store(GROUPS - 1)

        @block.gpsimd
        def _(pool):
            for tile, value in [(x_in[:, :, :], 0.0), (sel[:, :, :, :], 0.0), (minus_half[:, :], -0.5),
                                (p2[:, :, :], 0.0), (gates3[:, :, :], 0.0), (yT[:, :], 0.0), (ones[:, :], 1.0),
                                (euler[:, :, :], EULER)]:
                pool.memset(tile, value).then_inc(zeroed, 1)
            pool.wait_ge(zeroed, N_ZEROED)
            with pool.Fori(0, GROUPS) as g:
                for kind, *at in SCHEDULE:
                    if kind == "stats":
                        n, p = at
                        pool.wait_ge(var_done, due(g, kind, *at))
                        pool.tensor_tensor(rstd[:, pslice(p)], var[:, pslice(p)], minus_half[:, pslice(p)], ALU.pow
                                           ).then_inc(rstd_done, 1)
                    elif kind == "lg":
                        layer, p = at
                        n = E + layer
                        pool.wait_ge(lg_sub, due(g, kind, *at))
                        pool.tensor_tensor(lg[:, pslice(p), 0:n], euler[:, :, 0:n], lg[:, pslice(p), 0:n], ALU.pow
                                           ).then_inc(lg_exp, 1)
                    elif kind == "gate":
                        p, = at
                        await_copy(pool, g, f"s2c{p}")
                        await_copy(pool, g, f"c2s{p}")
                        pool.tensor_tensor(part_of(diff, p), part_of(c2sT, p), part_of(s2cT, p), ALU.subtract
                                           ).then_inc(diff_done, 1)

        @block.tensor
        def _(pe):
            pe.wait_ge(w_in, 16 * N_LOADS["w"])
            pe.wait_ge(zeroed, N_ZEROED)
            pe.wait_ge(setup, N_SETUP - 1)
            pe.matmul(ps[:, 0, 0:HALF], ones[0:S, :], any_diag[0:S, :], start=True, stop=True).then_inc(any_filled, 1)
            pe.wait_ge(setup, N_SETUP)

            def transposes(g, name, tiles, rows_out=128):
                await_bank(pe, g, name)
                for k, t in enumerate(tiles):
                    mm = pe.transpose(ring(name)[0:rows_out, k * 128:(k + 1) * 128], t, W["ident"])
                mm.then_inc(ring_filled, 1)

            def project(g, name, weight, source, of):
                await_ring(pe, g, name, copied=[of])
                pe.matmul(ring(name)[:, 0:source.shape[1]], weight, source, start=True, stop=True
                          ).then_inc(ring_filled, 1)

            def pair_scores(g, layer, s):
                if layer == 0:
                    pe.wait_ge(cols_loaded[s], 16 * g + 16)
                    await_copy(pe, g, f"qk{s // PP}")
                else:
                    await_copy(pe, g, f"qw{s // PP}")
                    if s == 0:
                        await_inner(pe, g, *[tile for tile in TILES if tile[0] == 0][-1])
                for c in range(3):
                    for half in range(2):
                        mm = pe.matmul(ps[HALF * half:HALF * half + HALF, c, 0:CHUNK],
                                       qk[:, s * PAIR + HALF * half:s * PAIR + HALF * half + HALF],
                                       cols[:, s, half, 4 * c:4 * c + 4, :], start=True, stop=True)
                mm.then_inc(scored, 1)

            def turn_probs(g, layer, s):
                pe.wait_ge(exp_done, due(g, "scores", layer, s))
                flat = prob[:, :, :].rearrange("p c n -> p (c n)")
                for c in range(3):
                    transposes(g, f"turn{layer}{s}.{c}",
                               [flat[:, (4 * c + k) * BR:(4 * c + k + 1) * BR] for k in range(4)], rows_out=BR)

            def context_sum(g, layer, s):
                if layer == 0:
                    pe.wait_ge(rows_loaded[s], 32 * g + 32)
                bank = ps[:, SUM_BANKS[s % 2], 0:D]
                if s >= 2:
                    pe.wait_ge(on_done, due(g, "sum", layer, s - 2))
                for j in range(BLOCKS):
                    if j % 4 == 0:
                        await_copy(pe, g, f"turn{layer}{s}.{j // 4}")
                    for half in range(2):
                        mm = pe.matmul(bank[HALF * half:HALF * half + HALF, :],
                                       pT[0:BR, j, HALF * half:HALF * half + HALF],
                                       rows[0:BR, s, half, j, :], start=(j == 0), stop=(j == BLOCKS - 1))
                mm.then_inc(summed, 1)

            def tile_products(g, layer, p, t):
                up, spread = [(up0, spread0), (up1, spread1)][layer]
                M, k = tile_rows(layer, t), TILES.index((layer, p, t))
                if k >= DEPTH and TILES[k - DEPTH][0] == layer:
                    await_inner(pe, g, *TILES[k - DEPTH])
                if k == 0:
                    pe.wait_ge(experts_in, 16 * N_LOADS["experts"])
                xs = real(part_of(xnT, p))
                bank = ps[0:M, k % DEPTH, :]
                await_copy(pe, g, f"xnT{2 * layer + 1}{p}")
                pe.matmul(bank[:, 0:PR], up[:, 0, t * 128:t * 128 + M], xs, start=True, stop=True)
                pe.matmul(bank[:, PR:2 * PR], up[:, 1, t * 128:t * 128 + M], xs, start=True, stop=True
                          ).then_inc(gu_filled, 1)
                if routed(layer, t):
                    name = f"g{layer}{p}.{t}"
                    await_ring(pe, g, name, copied=[f"gt{layer}{p}"])
                    pe.matmul(ring(name)[0:M, 0:PR], spread[:, t, 0:M], real(part_of(gatesT, p)),
                              start=True, stop=True).then_inc(ring_filled, 1)

            def down_product(g, layer, p, t):
                down = [down0, down1][layer]
                M = tile_rows(layer, t)
                first, last = (("down", layer, p, t) == which[layer, p] for which in (FIRST_DOWN, LAST_DOWN))
                if first:
                    pe.wait_ge(on_done, due(g, "sum", layer, PP + p))
                await_inner(pe, g, layer, p, t)
                mm = pe.matmul(ps[:, SUM_BANKS[p], 0:PR], down[0:M, t, :], h[0:M, in_flight(layer, p, t), :],
                               start=first, stop=last)
                if last:
                    mm.then_inc(y_done, 1)

            def step(g, kind, *at):
                if kind == "sel":
                    p, = at
                    if p == 0:
                        pe.wait_ge(sel_loaded, (g + 1) * 16 * 2 * PERIOD)
                    transposes(g, f"sel{p}", [sel[:, s, k, :] for s in pairs(p) for k in range(2)])
                elif kind == "qs":
                    p, = at
                    project(g, f"qs{p}", W["WqsT"], selT[:, p * 512:(p + 1) * 512], f"sel{p}")
                elif kind == "xnT":
                    n, p = at
                    pe.wait_ge(xn_done, due(g, "norm", n, p))
                    transposes(g, f"xnT{n}{p}", [xn[:, s, :] for s in pairs(p)])
                elif kind == "q":
                    project(g, f"q{at[0]}", W["WqcT"], part_of(xnT, at[0]), f"xnT0{at[0]}")
                elif kind == "kc":
                    project(g, f"kc{at[0]}", W["WkcT"], part_of(xnT, at[0]), f"xnT0{at[0]}")
                elif kind == "qk":
                    p, = at
                    name = f"qk{p}"
                    await_ring(pe, g, name, copied=[f"q{p}"])
                    pe.matmul(ring(name)[:, 0:PT], W["Wks"], part_of(qT, p), start=True, stop=True)
                    for k, s in enumerate(pairs(p)):
                        mm = pe.matmul(ring(name)[:, PT + k:PT + k + 1], qT[:, s * PAIR:(s + 1) * PAIR], Bc["bk_s"],
                                       start=True, stop=True)
                    mm.then_inc(ring_filled, 1)
                elif kind == "vc":
                    p, = at
                    await_ring(pe, g, f"vc{p}", copied=[f"xnT0{p}"])
                    for k, s in enumerate(pairs(p)):
                        mm = pe.matmul(ring(f"vc{p}")[:, k * D:(k + 1) * D], xnT[:, s * PAIR:(s + 1) * PAIR],
                                       W["WvcT"], start=True, stop=True)
                    mm.then_inc(ring_filled, 1)
                elif kind == "s2":
                    p, = at
                    name = f"s2{p}"
                    await_ring(pe, g, name, copied=[f"qs{p}", f"kc{p}"])
                    for k in range(2 * PP):
                        s = p * PP + k // 2
                        mm = pe.matmul(ring(name)[:, k * 128:(k + 1) * 128], qsT[:, 2 * PP * p + k, :],
                                       kcT[:, s * PAIR:(s + 1) * PAIR], start=True, stop=True)
                    mm.then_inc(ring_filled, 1)
                elif kind == "p2":
                    p, = at
                    pe.wait_ge(s2_mix, due(g, "s2mix", p))
                    transposes(g, f"p2{p}", [p2[:, s, :] for s in pairs(p)])
                elif kind == "s2c":
                    p, = at
                    await_ring(pe, g, f"s2c{p}", copied=[f"p2{p}", f"vc{p}"])
                    for k, s in enumerate(pairs(p)):
                        mm = pe.matmul(ring(f"s2c{p}")[:, k * D:(k + 1) * D], vc[:, s, :],
                                       p2T[:, s * PAIR:(s + 1) * PAIR], start=True, stop=True)
                    mm.then_inc(ring_filled, 1)
                elif kind == "scores":
                    pair_scores(g, *at)
                elif kind == "turn":
                    turn_probs(g, *at)
                elif kind == "sum":
                    context_sum(g, *at)
                elif kind == "on":
                    layer, p = at
                    pe.wait_ge(on_done, due(g, "sum", layer, PP * p + PP - 1))
                    transposes(g, f"on{layer}{p}", [on[:, s, :] for s in pairs(p)])
                elif kind == "c2s":
                    project(g, f"c2s{at[0]}", W["WvsT"], part_of(onT, at[0]), f"on0{at[0]}")
                elif kind == "gate":
                    p, = at
                    out = ring(f"gate{p}")[:, 0:PT]
                    await_ring(pe, g, f"gate{p}", copied=[f"s2c{p}", f"c2s{p}"])
                    pe.matmul(out, W["WgaT"], part_of(c2sT, p), start=True, stop=False)
                    pe.matmul(out, W["WgbT"], part_of(s2cT, p), start=False, stop=True).then_inc(ring_filled, 1)
                elif kind == "dx":
                    p, = at
                    pe.wait_ge(mixed, due(g, "mix", p))
                    transposes(g, f"dx{p}", [gate[:, s * PAIR:(s + 1) * PAIR] for s in pairs(p)])
                elif kind == "lg":
                    layer, p = at
                    weight, n = [(router[:, 0:E], E), (router[:, E:2 * E + 1], E + 1)][layer]
                    name = f"lg{layer}{p}"
                    await_ring(pe, g, name, copied=[f"xnT{2 * layer + 1}{p}"])
                    for k, s in enumerate(pairs(p)):
                        mm = pe.matmul(ring(name)[:, k * n:(k + 1) * n], xnT[:, s * PAIR:(s + 1) * PAIR], weight,
                                       start=True, stop=True)
                    mm.then_inc(ring_filled, 1)
                elif kind == "gt":
                    layer, p = at
                    name = f"gt{layer}{p}"
                    pe.wait_ge(gates_done, due(g, "gates", layer, p))
                    await_bank(pe, g, name)
                    for k, s in enumerate(pairs(p)):
                        mm = pe.transpose(ring(name).bitcast(BF16)[0:GATE_ROWS, k * 128:(k + 1) * 128],
                                          gates3[:, s, :], identb[:, :])
                    mm.then_inc(ring_filled, 1)
                elif kind == "tile":
                    tile_products(g, *at)
                elif kind == "down":
                    down_product(g, *at)
                elif kind == "yT":
                    layer, p = at
                    pe.wait_ge(y_copied, due(g, "y", layer, p))
                    transposes(g, f"yT{layer}{p}", [yT[:, s * PAIR:(s + 1) * PAIR] for s in pairs(p)])
                elif kind == "q1":
                    project(g, f"q1{at[0]}", W["wi"], part_of(xnT, at[0]), f"xnT2{at[0]}")
                elif kind == "qw":
                    project(g, f"qw{at[0]}", W["wiT"], part_of(qT, at[0]), f"q1{at[0]}")
                elif kind == "o1":
                    p, = at
                    await_ring(pe, g, f"o1{p}", copied=[f"on1{p}"])
                    for k, s in enumerate(pairs(p)):
                        bank = ring(f"o1{p}")[:, k * D:(k + 1) * D]
                        pe.matmul(bank, xnT[:, s * PAIR:(s + 1) * PAIR], W["wi"], start=True, stop=False)
                        mm = pe.matmul(bank, onT[:, s * PAIR:(s + 1) * PAIR], W["wi"], start=False, stop=True)
                    mm.then_inc(ring_filled, 1)

            with pe.Fori(0, GROUPS) as g:
                for kind, *at in SCHEDULE:
                    step(g, kind, *at)

        @block.scalar
        def _(act):
            for dst, src in [
                (w[:, :, :], d["w"]), (bias[:, :], d["bias"]),
                (bv_c_row[:, :], d["bv_c"].partition_broadcast(128)),
                (gate_bias[:, :], d["gate_bias"].partition_broadcast(128)),
                (router[:, :], d["router"]),
                (identb[:, :], d["identb"]),
                (least_lead[:, :, :].rearrange("p e j -> p (e j)"), d["least_lead"].partition_broadcast(128)),
                (w_interp[:, :], d["w_interp"]),
            ]:
                act.dma_start(dst, src).then_inc(w_in, 16)
            for half in range(2):
                act.dma_start(mask_u8[HALF * half:HALF * half + S, :], d["mask"]).then_inc(mask_in, 16)
            for dst, src in [
                (up0[:, :, :], d["up0"]), (down0[:, :, :], d["down0"]), (spread0[:, :, :], d["spread0"]),
                (up1[:, :, :], d["up1"]), (down1[:, 0:L1_TILES - 1, :], d["down1"][:, 0:L1_TILES - 1, :]),
                (down1[0:L1_ROWS % 128, L1_TILES - 1, :], d["down1"][0:L1_ROWS % 128, L1_TILES - 1, :]),
                (spread1[:, :, :], d["spread1"]),
            ]:
                act.dma_start(dst, src).then_inc(experts_in, 16)
            act.wait_ge(w_in, 16 * N_LOADS["w"])
            act.wait_ge(setup, N_SETUP)
            act.wait_ge(zeroed, N_ZEROED)

            def copy(g, name, out, bias=None):
                act.wait_ge(ring_filled, filled(g, name))
                source = ring(name)[0:out.shape[0], 0:out.shape[1]]
                if bias is None:
                    act.copy(out, source).then_inc(emptied(name), 1)
                else:
                    act.activation(out, source, ACT.Identity, bias=bias).then_inc(emptied(name), 1)

            def step(g, kind, *at):
                if kind == "sel":
                    copy(g, f"sel{at[0]}", selT[:, at[0] * 512:(at[0] + 1) * 512])
                elif kind == "qs":
                    p, = at
                    copy(g, f"qs{p}", qsT[:, 2 * PP * p:2 * PP * (p + 1), :].rearrange("p a b -> p (a b)"),
                         bias=Bc["bq_s"])
                elif kind == "xnT":
                    n, p = at
                    copy(g, f"xnT{n}{p}", part_of(xnT, p))
                elif kind == "q":
                    copy(g, f"q{at[0]}", part_of(qT, at[0]), bias=Bc["bq_c"])
                elif kind == "q1":
                    copy(g, f"q1{at[0]}", part_of(qT, at[0]))
                elif kind == "scores":
                    layer, s = at
                    act.wait_ge(max_done, due(g, kind, *at))
                    act.activation(prob[:, :, :], scores if layer == 0 else prob[:, :, :], ACT.Exp,
                                   bias=ntop[:, s:s + 1], accum_out=total[:, s:s + 1]).then_inc(exp_done, 1)
                elif kind == "s2exp":
                    p, = at
                    both = s2[:, 2 * PP * p:2 * PP * (p + 1), :]
                    act.wait_ge(s2_sub, due(g, "s2", p))
                    act.activation(both, both, ACT.Exp).then_inc(s2_exp, 1)
                elif kind == "p2":
                    copy(g, f"p2{at[0]}", part_of(p2T, at[0]))
                elif kind == "s2c":
                    copy(g, f"s2c{at[0]}", part_of(s2cT, at[0]))
                elif kind == "turn":
                    layer, s = at
                    for c in (0, 1):
                        copy(g, f"turn{layer}{s}.{c}", pT[0:BR, 4 * c:4 * c + 4, :].rearrange("p j t -> p (j t)"))
                elif kind == "on":
                    layer, p = at
                    copy(g, f"on{layer}{p}", part_of(onT, p))
                elif kind == "gate":
                    p, = at
                    act.wait_ge(ring_filled, filled(g, f"gate{p}"))
                    act.activation(part_of(gate, p), ring(f"gate{p}")[:, 0:PT], ACT.Tanh, bias=half_bg[:, 0:1],
                                   scale=0.5).then_inc(emptied(f"gate{p}"), 1)
                elif kind == "tile":
                    layer, p, t = at
                    M, k = tile_rows(layer, t), in_flight(layer, p, t)
                    act.wait_ge(gu_filled, due(g, kind, *at))
                    act.activation(sg[0:M, k, :], ps[0:M, k, 0:PR], ACT.Silu).then_inc(silu_done, 1)
                elif kind == "y":
                    layer, p = at
                    act.wait_ge(y_done, due(g, kind, *at))
                    act.copy(real(part_of(yT, p)), ps[:, SUM_BANKS[p], 0:PR].rearrange("p (n q) -> p n q", q=S)
                             ).then_inc(y_copied, 1)

            with act.Fori(0, GROUPS) as g:
                for kind, *at in SCHEDULE:
                    step(g, kind, *at)

        @block.vector
        def _(dve):
            def wait_apart(semaphore, value):
                dve.wait_ge(semaphore, value)
                dve.sem_inc(apart, 1)

            class Steps:
                def __init__(self, semaphore, count):
                    self.semaphore, self.count, self.g, self.n = semaphore, count, 0, 0

                def start(self, g):
                    self.g, self.n = g, 0

                def step(self, instruction):
                    instruction.then_inc(self.semaphore, 1)
                    self.n += 1
                    dve.wait_ge(self.semaphore, self.g * self.count + self.n)

                def step_apart(self, instruction):
                    instruction.then_inc(self.semaphore, 1)
                    self.n += 1
                    wait_apart(self.semaphore, self.g * self.count + self.n)

            own = Steps(dve_step, DVE_STEPS)
            first = Steps(setup, N_SETUP)

            first.step(dve.memset(penalty[:, :, :], 0.0))
            dve.wait_ge(w_in, 16 * N_LOADS["w"])
            first.step(dve.tensor_scalar(half_bg[:, :], Bc["bg"], 0.5, None, ALU.mult))
            dve.wait_ge(mask_in, 16 * N_LOADS["mask"])
            for half in range(2):
                q = slice(HALF * half, HALF * half + S)
                first.step(dve.tensor_scalar(penalty[q, :, :].rearrange("p c (j r) -> p (c j) r", j=4),
                                             mask_u8[q, :].rearrange("p (r j) -> p j r", j=BLOCKS),
                                             -1.0, -MASKED, ALU.add, ALU.mult))
            first.step(dve.tensor_reduce(any_col[0:S, :], mask_u8[0:S, :], X, ALU.max))
            first.step(dve.tensor_scalar(any_diag[0:S, :], W["ident"][0:S, 0:HALF], any_col[0:S, 0:1], None, ALU.mult))
            dve.wait_ge(any_filled, 1)
            for b in range(3):
                dve.sem_inc(ring_free[b], 1)
            first.step(dve.tensor_copy(any_row[:, :], ps[:, 0, 0:HALF]))
            assert first.n == N_SETUP, first.n

            def wait_filled(g, name):
                dve.wait_ge(ring_filled, filled(g, name))

            def as_pairs(name):
                return ring(name)[:, 0:PT].rearrange("p (s e) -> p s e", s=PP)

            def add_to_x(g, name, p):
                wait_filled(g, name)
                dve.tensor_tensor(x[:, pslice(p), :], x[:, pslice(p), :], as_pairs(name), ALU.add
                                  ).then_inc(emptied(name), 1)
                await_copy(dve, g, name)

            def halves():
                return [slice(HALF * h, HALF * h + HALF) for h in range(2)]

            def small_scores(g, p):
                name = f"s2{p}"
                span = slice(2 * PP * p, 2 * PP * (p + 1))
                wait_filled(g, name)
                blocks = ring(name).rearrange("p (k t) -> p k t", k=2 * PP)
                for hs in halves():
                    ins = dve.tensor_copy(s2[hs, span, :], blocks[hs, :, hs.start:hs.start + S])
                ins.then_inc(emptied(name), 1)
                await_copy(dve, g, name)
                own.step(dve.tensor_reduce(s2max[:, span], s2[:, span, :], X, ALU.max))
                dve.tensor_tensor(s2[:, span, :], s2[:, span, :],
                                  s2max[:, span].unsqueeze(2).to_broadcast([128, 2 * PP, S]),
                                  ALU.subtract).then_inc(s2_sub, 1)

            def small_mix(g, p):
                span = slice(2 * PP * p, 2 * PP * (p + 1))
                dve.wait_ge(s2_exp, due(g, "s2exp", p))
                own.step(dve.tensor_reduce(s2sum[:, span], s2[:, span, :], X, ALU.add))
                own.step(dve.reciprocal(coef[:, span], s2sum[:, span]))
                own.step(dve.tensor_tensor(coef[:, span], coef[:, span], w_interp[:, span], ALU.mult))
                own.step(dve.tensor_tensor(s2[:, span, :], s2[:, span, :],
                                           coef[:, span].unsqueeze(2).to_broadcast([128, 2 * PP, S]), ALU.mult))
                both = s2[:, span, :].rearrange("p (s w) k -> p s w k", w=2)
                for hs in halves():
                    ins = dve.tensor_tensor(p2[hs, pslice(p), hs.start:hs.start + S],
                                            both[hs, :, 0, :], both[hs, :, 1, :], ALU.add)
                ins.then_inc(s2_mix, 1)

            def step(g, kind, *at):
                if kind == "take":
                    dve.wait_ge(x_loaded, 32 * g + 32)
                    dve.tensor_copy(x[:, :, :], x_in[:, :, :]).then_inc(x_taken, 1)
                    dve.wait_ge(x_taken, g + 1)
                elif kind == "stats":
                    n, p = at
                    for s in pairs(p):
                        ins = dve.bn_stats(stats[:, s, :], x[:, s, :])
                    own.step_apart(ins)
                    for s in pairs(p):
                        ins = dve.bn_aggr(mv[:, s, :], stats[:, s, :])
                    own.step(ins)
                    dve.tensor_scalar(var[:, pslice(p)], mv[:, pslice(p), 1], EPS, None, ALU.add).then_inc(var_done, 1)
                elif kind == "norm":
                    n, p = at
                    dve.wait_ge(rstd_done, due(g, "stats", n, p))
                    for s in pairs(p):
                        ins = dve.tensor_scalar(xn[:, s, :], x[:, s, :], mv[:, s, 0:1], rstd[:, s:s + 1],
                                                ALU.subtract, ALU.mult)
                    ins.then_inc(xn_done, 1)
                elif kind == "qk":
                    p, = at
                    name = f"qk{p}"
                    wait_filled(g, name)
                    dve.tensor_scalar(minus_qb[:, pslice(p)], ring(name)[:, PT:PT + PP], -SCALE, None, ALU.mult)
                    dve.tensor_scalar(part_of(qk, p), ring(name)[:, 0:PT], SCALE, None, ALU.mult
                                      ).then_inc(emptied(name), 1)
                    await_copy(dve, g, name)
                elif kind == "kc":
                    p, = at
                    wait_filled(g, f"kc{p}")
                    dve.tensor_scalar(part_of(kcT, p), ring(f"kc{p}")[:, 0:PT], Bc["bk_c"], SCALE, ALU.add, ALU.mult
                                      ).then_inc(emptied(f"kc{p}"), 1)
                elif kind == "vc":
                    p, = at
                    wait_filled(g, f"vc{p}")
                    dve.tensor_tensor(vc[:, pslice(p), :], as_pairs(f"vc{p}"),
                                      bv_c_row[:, :].unsqueeze(1).to_broadcast([128, PP, D]), ALU.add
                                      ).then_inc(emptied(f"vc{p}"), 1)
                elif kind == "s2":
                    small_scores(g, *at)
                elif kind == "s2mix":
                    small_mix(g, *at)
                elif kind == "scores":
                    layer, s = at
                    if layer == 0:
                        dve.wait_ge(scored, due(g, kind, *at))
                        own.step(dve.tensor_reduce(top[:, s:s + 1], scores, mybir.AxisListType.XY, ALU.max,
                                                   negate=True))
                        dve.scalar_tensor_tensor(out=ntop[:, s:s + 1], in0=top[:, s:s + 1],
                                                 scalar=minus_qb[:, s:s + 1], in1=minus_qb[:, s:s + 1],
                                                 op0=ALU.add, op1=ALU.subtract).then_inc(max_done, 1)
                    else:
                        wait_apart(scored, due(g, kind, *at))
                        own.step(dve.tensor_tensor_reduce(prob[:, :, :], scores, penalty[:, :, :], 1.0, LOWEST,
                                                          ALU.add, ALU.max, top[:, s:s + 1]))
                        dve.tensor_scalar(ntop[:, s:s + 1], top[:, s:s + 1], -1.0, None, ALU.mult
                                          ).then_inc(max_done, 1)
                elif kind == "turn":
                    layer, s = at
                    name = f"turn{layer}{s}.2"
                    wait_filled(g, name)
                    dve.tensor_copy(pT[0:BR, 8:12, :].rearrange("p j t -> p (j t)"), ring(name)[0:BR, :]
                                    ).then_inc(emptied(name), 1)
                elif kind == "sum":
                    layer, s = at
                    dve.wait_ge(exp_done, due(g, "scores", layer, s))
                    own.step(dve.reciprocal(rtotal[:, s:s + 1], total[:, s:s + 1]))
                    dve.wait_ge(summed, due(g, kind, *at))
                    dve.tensor_scalar(on[:, s, :], ps[:, SUM_BANKS[s % 2], 0:D], rtotal[:, s:s + 1], None, ALU.mult
                                      ).then_inc(on_done, 1)
                elif kind == "c2s":
                    p, = at
                    wait_filled(g, f"c2s{p}")
                    dve.tensor_scalar(part_of(c2sT, p), ring(f"c2s{p}")[:, 0:PT], Bc["bv_s"], None, ALU.add
                                      ).then_inc(emptied(f"c2s{p}"), 1)
                elif kind == "mix":
                    p, = at
                    out = part_of(gate, p)
                    dve.wait_ge(diff_done, due(g, "gate", p))
                    await_copy(dve, g, f"gate{p}")
                    own.step(dve.scalar_tensor_tensor(out=out, in0=out, scalar=1.0, in1=part_of(diff, p),
                                                      op0=ALU.add, op1=ALU.mult))
                    dve.scalar_tensor_tensor(out=out, in0=out, scalar=0.5, in1=part_of(s2cT, p),
                                             op0=ALU.mult, op1=ALU.add).then_inc(mixed, 1)
                elif kind in ("dx", "o1"):
                    add_to_x(g, f"{kind}{at[0]}", at[0])
                elif kind == "lg":
                    layer, p = at
                    n = E + layer
                    name = f"lg{layer}{p}"
                    wait_filled(g, name)
                    z = ring(name)[:, 0:PP * n].rearrange("p (s e) -> p s e", s=PP)
                    own.step(dve.tensor_reduce(lmax[:, pslice(p)], z[:, :, 0:E], X, ALU.max))
                    if layer:
                        dve.tensor_scalar(lg[:, pslice(p), E:E + 1], z[:, :, E:E + 1], -1.0, None, ALU.mult)
                    dve.tensor_tensor(lg[:, pslice(p), 0:E], z[:, :, 0:E],
                                      lmax[:, pslice(p)].unsqueeze(2).to_broadcast([128, PP, E]),
                                      ALU.subtract).then_inc(emptied(name), 1)
                    await_copy(dve, g, name)
                    dve.sem_inc(lg_sub, 1)
                elif kind == "softmax":
                    layer, p = at
                    score = lg[:, pslice(p), 0:E]
                    dve.wait_ge(lg_exp, due(g, "lg", layer, p))
                    own.step(dve.tensor_reduce(lsum[:, pslice(p)], score, X, ALU.add))
                    own.step(dve.reciprocal(lsum[:, pslice(p)], lsum[:, pslice(p)]))
                    own.step(dve.tensor_tensor(score, score, lsum[:, pslice(p)].unsqueeze(2).to_broadcast([128, PP, E]),
                                               ALU.mult))
                    if layer == 0:
                        own.step(dve.tensor_tensor(key[:, pslice(p), :], score,
                                                   gate_bias[:, :].unsqueeze(1).to_broadcast([128, PP, E]), ALU.add))
                    else:
                        shared = gates[:, pslice(p), E:E + 1]
                        own.step(dve.tensor_scalar(shared, lg[:, pslice(p), E:E + 1], 1.0, None, ALU.add))
                        own.step(dve.reciprocal(shared, shared))
                elif kind == "rank":
                    layer, p = at
                    k = key[:, pslice(p), :] if layer == 0 else lg[:, pslice(p), 0:E]
                    shape = [128, PP, E, E]
                    mine, other = k.unsqueeze(3).to_broadcast(shape), k.unsqueeze(2).to_broadcast(shape)
                    own.step(dve.tensor_tensor(lead[p], other, mine, ALU.subtract))
                    own.step(dve.tensor_tensor(lead[p], lead[p], least_lead[:, :, :].unsqueeze(1).to_broadcast(shape),
                                               ALU.is_ge))
                    own.step(dve.tensor_reduce(rank[:, pslice(p), :], lead[p], X, ALU.add))
                elif kind == "gates":
                    layer, p = at
                    n = E + layer
                    own.step(dve.scalar_tensor_tensor(out=gates[:, pslice(p), 0:E], in0=rank[:, pslice(p), :],
                                                      scalar=2.0, in1=lg[:, pslice(p), 0:E],
                                                      op0=ALU.is_lt, op1=ALU.mult))
                    left = gates[:, pslice(p), 0:n]
                    for part in range(3):
                        cut = gates3[:, pslice(p), 32 * part:32 * part + n]
                        ins = dve.tensor_copy(cut, left)
                        if part < 2:
                            own.step(ins)
                            own.step(dve.tensor_tensor(rest[:, pslice(p), 0:n], left, cut, ALU.subtract))
                            left = rest[:, pslice(p), 0:n]
                    ins.then_inc(gates_done, 1)
                elif kind == "gt":
                    layer, p = at
                    name = f"gt{layer}{p}"
                    wait_filled(g, name)
                    dve.tensor_copy(part_of(gatesT, p), ring(name).bitcast(BF16)[0:GATE_ROWS, 0:PT]
                                    ).then_inc(emptied(name), 1)
                elif kind == "tile":
                    layer, p, t = at
                    M, k = tile_rows(layer, t), in_flight(layer, p, t)
                    out = (hu if routed(layer, t) else h)[0:M, k, :]
                    if routed(layer, t):
                        name = f"g{layer}{p}.{t}"
                        wait_filled(g, name)
                    dve.wait_ge(silu_done, due(g, kind, *at))
                    ins = dve.tensor_tensor(out, sg[0:M, k, :], ps[0:M, k, PR:2 * PR], ALU.mult)
                    if routed(layer, t):
                        own.step(ins)
                        dve.tensor_tensor(h[0:M, k, :], out, ring(name)[0:M, 0:PR], ALU.mult
                                          ).then_inc(emptied(name), 1)
                    else:
                        ins.then_inc(h_done, 1)
                elif kind == "yT" and at[0] == 0:
                    add_to_x(g, f"yT0{at[1]}", at[1])
                elif kind == "yT":
                    p = at[1]
                    name = f"yT1{p}"
                    wait_filled(g, name)
                    if p == 0:
                        dve.wait_ge(out_free, g + 1)
                    dve.tensor_tensor(x_out[:, pslice(p), :], x[:, pslice(p), :], as_pairs(name), ALU.add
                                      ).then_inc(emptied(name), 1)
                    await_copy(dve, g, name)
                elif kind == "qw":
                    p, = at
                    name = f"qw{p}"
                    wait_filled(g, name)
                    dve.scalar_tensor_tensor(out=part_of(qk, p).rearrange("p (n q) -> p n q", q=HALF),
                                             in0=ring(name)[:, 0:PT].rearrange("p (n q) -> p n q", q=HALF),
                                             scalar=SCALE,
                                             in1=any_row[:, :].unsqueeze(1).to_broadcast([128, 2 * PP, HALF]),
                                             op0=ALU.mult, op1=ALU.mult).then_inc(emptied(name), 1)

            with dve.Fori(0, GROUPS) as g:
                own.start(g)
                for kind, *at in SCHEDULE:
                    step(g, kind, *at)
                assert own.n == DVE_STEPS, own.n


def kernel(**inputs):
    import ml_dtypes
    import numpy as np
    import concourse.bacc as bacc
    from concourse.bass_utils import run_bass_kernel_spmd

    a = {k: np.asarray(v) for k, v in inputs.items()}
    f32 = np.float32

    def T(name):
        return a[name].T

    def side(*blocks):
        return np.concatenate(blocks, axis=1)

    def tiles(m):
        m = np.concatenate([m, np.zeros((-len(m) % 128, m.shape[1]), m.dtype)], axis=0)
        return m.reshape(-1, 128, m.shape[1]).transpose(1, 0, 2)

    _, _, w_hi = interpolation()
    w_interp = np.zeros((128, PAIRS, 2), f32)
    for half in range(2):
        w_interp[HALF * half:HALF * half + S, :, 0] = (f32(1) - w_hi)[:, None]
        w_interp[HALF * half:HALF * half + S, :, 1] = w_hi[:, None]

    def spread(rows_of_gate, n_tiles):
        m = np.zeros((GATE_ROWS, n_tiles, 128), ml_dtypes.bfloat16)
        for r, gate in enumerate(rows_of_gate):
            for part in range(3):
                m[32 * part + gate, r // 128, r % 128] = 1
        return m

    Wg = a["L0_xattn_Wg"]
    attention = {
        "WqcT": T("L0_xattn_Wq_c"), "Wks": a["L0_xattn_Wk_s"], "WvsT": T("L0_xattn_Wv_s"),
        "WqsT": T("L0_xattn_Wq_s"), "WkcT": T("L0_xattn_Wk_c"), "WvcT": T("L0_xattn_Wv_c"),
        "WgaT": Wg[:, :D].T, "WgbT": Wg[:, D:].T, "wi": a["L1_xattn_wi"], "wiT": T("L1_xattn_wi"),
        "ident": np.eye(128, dtype=f32),
    }
    w1, w3, w2 = a["L0_ffn_w1"], a["L0_ffn_w3"], a["L0_ffn_w2"]
    gu, dn = a["L1_ffn_experts_gate_up"], a["L1_ffn_experts_down"]
    arrays = {
        "x": a["x"], "ctx": a["ctx_1024"],
        "ctxT": a["ctx_1024"].reshape(BATCH, BR, BLOCKS, D).transpose(0, 3, 2, 1).reshape(BATCH, D, S2),
        "mask": a["mask_1xSxS2_bk0"][0],
        "w": np.stack([attention[n] for n in W_NAMES], axis=1),
        "bias": np.stack([a["L0_xattn_" + n] for n in B_NAMES], axis=1),
        "bv_c": a["L0_xattn_bv_c"], "gate_bias": a["L0_ffn_gate_bias"],
        "router": side(T("L0_ffn_gate_w"), T("L1_ffn_gate_w"), T("L1_ffn_shared_expert_gate_w")),
        "identb": np.eye(128, dtype=ml_dtypes.bfloat16),
        "least_lead": np.where(np.tril(np.ones((E, E)), -1) > 0, f32(0), np.finfo(f32).tiny).astype(f32).reshape(-1),
        "w_interp": w_interp.reshape(128, -1),
        "up0": np.stack([side(*[m.T for m in w1], T("L0_ffn_sw1")), side(*[m.T for m in w3], T("L0_ffn_sw3"))], axis=1),
        "down0": tiles(np.concatenate([*[m.T for m in w2], T("L0_ffn_sw2")], axis=0)),
        "spread0": spread(np.arange(E * 128) // 128, E),
        "up1": np.stack([side(*[m[:I1].T for m in gu], T("L1_ffn_shared_gate_w")),
                         side(*[m[I1:].T for m in gu], T("L1_ffn_shared_up_w"))], axis=1),
        "down1": tiles(np.concatenate([*[m.T for m in dn], T("L1_ffn_shared_down_w")], axis=0)),
        "spread1": spread(np.minimum(np.arange(L1_ROWS) // I1, E), L1_TILES),
    }
    nc = bacc.Bacc("TRN2", target_bir_lowering=False, num_devices=1)
    given, dram = {}, {}
    for name, array in arrays.items():
        given["in_" + name] = np.ascontiguousarray(array)
        dram[name] = nc.dram_tensor("in_" + name, array.shape, mybir.dt.from_np(array.dtype), kind="ExternalInput").ap()
    dram["out"] = nc.dram_tensor("out_0", (BATCH, S, D), F32, kind="ExternalOutput").ap()
    build(nc, dram)
    return run_bass_kernel_spmd(nc, [given], core_ids=[0]).results[0]["out_0"]
```

```python
from contextlib import ExitStack

import concourse.bass as bass
from concourse import mybir

F32 = mybir.dt.float32
BF16 = mybir.dt.bfloat16
U8 = mybir.dt.uint8
ALU = mybir.AluOpType
ACT = mybir.ActivationFunctionType
X = mybir.AxisListType.X

BATCH, S, D, S2 = 32, 56, 128, 1500
HALF = 64
PAIR = 2 * HALF
PAIRS = 4
GROUPS = BATCH // (2 * PAIRS)
GT = PAIRS * PAIR
PARTS = 2
PP = PAIRS // PARTS
PT = PP * PAIR
PR = PP * 2 * S
BLOCKS = 12
BR = S2 // BLOCKS
MAIN = 112
BANK = 512
CHUNK = S2 // 3
E = 8
EPS = 1e-5
EULER = 2.718281828459045
SCALE = float(D) ** -0.5
MASKED = -1e10
LOWEST = -3.0e38

L0_TILES = E + 2
I1, SI1 = 176, 352
L1_ROWS = E * I1 + SI1
L1_TILES = -(-L1_ROWS // 128)
GATE_ROWS = 96

W_NAMES = ["Wqc", "Wks", "WvsT", "WqsT", "WkcT", "WgaT", "WgbT", "wi", "wiT", "ident", "WvcT"]
B_NAMES = ["bq_c", "bk_c", "bq_s", "bv_s", "bg", "bk_s"]

RING = [3, 4, 5]
SUM_BANKS = [6, 7]
DEPTH = 3


STEPS = """
    kc:1 turn:0,0 scores:0,1 sel:0 sel:1 sum:0,0 turn:0,1 qs:0 scores:0,2 s2:0 s2exp:0 s2mix:0 qs:1 sum:0,1
    turn:0,2 s2:1 on:0,0 p2:0 s2exp:1 scores:0,3 s2mix:1 s2c:0 c2s:0 sum:0,2 gate:0 mix:0 turn:0,3 dx:0
    stats:1,0 norm:1,0 sum:0,3 xnT:1,0 p2:1 on:0,1 lg:0,0 c2s:1 softmax:0,0 rank:0,0 gates:0,0 s2c:1 gate:1
    mix:1 tile:0,0,8 gt:0,0 tile:0,0,9 dx:1 stats:1,1 tile:0,0,0 norm:1,1 down:0,0,8 down:0,0,9 tile:0,0,1
    tile:0,0,2 down:0,0,0 xnT:1,1 tile:0,0,3 down:0,0,1 lg:0,1 down:0,0,2 tile:0,0,4 down:0,0,3 tile:0,0,5
    tile:0,1,8 down:0,0,4 softmax:0,1 rank:0,1 tile:0,0,6 down:0,0,5 down:0,1,8 tile:0,1,9 gates:0,1
    tile:0,0,7 down:0,0,6 down:0,1,9 gt:0,1 tile:0,1,0 down:0,0,7 y:0,0 tile:0,1,1 tile:0,1,2 yT:0,0
    down:0,1,0 tile:0,1,3 down:0,1,1 down:0,1,2 stats:2,0 tile:0,1,4 norm:2,0 tile:0,1,5 down:0,1,3 tile:0,1,6
    down:0,1,4 xnT:2,0 tile:0,1,7 down:0,1,5 qw:0 down:0,1,6 down:0,1,7 y:0,1 scores:1,0 yT:0,1 stats:2,1
    turn:1,0 norm:2,1 scores:1,1 xnT:2,1 sum:1,0 qw:1 turn:1,1 scores:1,2 sum:1,1 turn:1,2 on:1,0 scores:1,3
    o1:0 stats:3,0 norm:3,0 sum:1,2 xnT:3,0 turn:1,3 lg:1,0 softmax:1,0 rank:1,0 gates:1,0 sum:1,3 gt:1,0
    tile:1,0,0 on:1,1 tile:1,0,1 tile:1,0,2 o1:1 down:1,0,0 down:1,0,1 stats:3,1 tile:1,0,3 norm:3,1
    down:1,0,2 tile:1,0,4 tile:1,0,5 xnT:3,1 down:1,0,3 lg:1,1 +stats:0,0 tile:1,0,6 down:1,0,4 tile:1,0,7
    down:1,0,5 tile:1,0,8 down:1,0,6 softmax:1,1 tile:1,0,9 rank:1,1 down:1,0,7 tile:1,0,10 gates:1,1
    down:1,0,8 tile:1,0,11 down:1,0,9 tile:1,0,12 down:1,0,10 gt:1,1 tile:1,0,13 down:1,0,11 tile:1,1,0
    down:1,0,12 tile:1,1,1 down:1,0,13 tile:1,1,2 down:1,1,0 +stats:0,1 tile:1,1,3 down:1,1,1 tile:1,1,4
    down:1,1,2 tile:1,1,5 down:1,1,3 y:1,0 +norm:0,0 tile:1,1,6 down:1,1,4 tile:1,1,7 down:1,1,5 down:1,1,6
    tile:1,1,8 down:1,1,7 +xnT:0,0 tile:1,1,9 +norm:0,1 tile:1,1,10 down:1,1,8 tile:1,1,11 down:1,1,9
    tile:1,1,12 down:1,1,10 tile:1,1,13 +qk:0 down:1,1,11 down:1,1,12 +xnT:0,1 down:1,1,13 y:1,1 +vc:0 yT:1,0
    yT:1,1 +scores:0,0 +kc:0 +qk:1 +vc:1
"""


def parse(word):
    kind, _, at = word.strip("+").partition(":")
    return (kind, *(map(int, at.split(",")) if at else ()))


SCHEDULE = [parse(word) for word in STEPS.split()]
EARLY = {parse(word) for word in STEPS.split() if word.startswith("+")}


def routed(layer, t):
    return layer == 1 or t < E


def fills_of(kind, *at):
    if kind in ("sel", "qs", "kc", "qk", "vc", "s2", "p2", "s2c", "c2s", "gate", "dx", "qw", "o1"):
        return [f"{kind}{at[0]}"]
    if kind in ("xnT", "on", "lg", "gt", "yT"):
        return [f"{kind}{at[0]}{at[1]}"]
    if kind == "turn":
        return [f"turn{at[0]}{at[1]}.{c}" for c in range(3)]
    if kind == "tile" and routed(at[0], at[2]):
        return [f"g{at[0]}{at[1]}.{at[2]}"]
    return []


NTH = {step: sum(other[0] == step[0] for other in SCHEDULE[:k]) + 1 for k, step in enumerate(SCHEDULE)}
PER = {kind: sum(step[0] == kind for step in SCHEDULE) for kind in {step[0] for step in SCHEDULE}}
AHEAD = {kind: sum(step[0] == kind for step in EARLY) for kind in PER}
assert len(NTH) == len(SCHEDULE)
assert all((step in EARLY) == (NTH[step] > PER[step[0]] - AHEAD[step[0]]) for step in SCHEDULE)
ORDER = [name for step in SCHEDULE for name in fills_of(*step)]
AT = {name: k for k, name in enumerate(ORDER)}
EARLY_FILLS = {name for step in EARLY for name in fills_of(*step)}
FIRST_EARLY = min(AT[name] for name in EARLY_FILLS)
FILLS = len(ORDER)
USES = [len(range(b, FILLS, 3)) for b in range(3)]
TILES = [step[1:] for step in SCHEDULE if step[0] == "tile"]
UNROUTED = [tile for tile in TILES if not routed(tile[0], tile[2])]
LAST_DOWN = {step[1:3]: step for step in SCHEDULE if step[0] == "down"}
FIRST_DOWN = {step[1:3]: step for step in reversed(SCHEDULE) if step[0] == "down"}
N_ZEROED = 9
N_SETUP = 4
DVE_STEPS = 136
DVE_EARLY = 6


def due(g, *step):
    return g * PER[step[0]] + (AHEAD[step[0]] + NTH[step] - (PER[step[0]] if step in EARLY else 0))


def in_flight(layer, part, t):
    return TILES.index((layer, part, t)) % DEPTH


def tile_rows(layer, t):
    return min(128, [L0_TILES * 128, L1_ROWS][layer] - 128 * t)


def interpolation():
    import numpy as np
    one = np.float32
    pos = (np.arange(S, dtype=one) + one(0.5)) * one(S2 / S) - one(0.5)
    pos = np.clip(pos, one(0), one(S2 - 1)).astype(one)
    lo = np.floor(pos).astype(np.int32)
    hi = np.minimum(lo + 1, S2 - 1)
    return lo, hi, (pos - lo.astype(one)).astype(one)


def build(nc, d):
    with ExitStack() as ctx:
        def sb(name, shape, dt=F32):
            return ctx.enter_context(nc.sbuf_tensor(name, shape, dt))

        def sem(name):
            return ctx.enter_context(nc.semaphore(name))

        w = sb("w", [128, len(W_NAMES) * D + 1])
        W = {n: w[:, i * D:(i + 1) * D] for i, n in enumerate(W_NAMES)}
        qb_weight = w[:, len(W_NAMES) * D:]
        WvcT_qb = w[:, (len(W_NAMES) - 1) * D:]
        bias = sb("bias", [128, len(B_NAMES)])
        Bc = {n: bias[:, i:i + 1] for i, n in enumerate(B_NAMES)}
        half_bg = sb("half_bg", [128, 1])
        bv_c_row = sb("bv_c_row", [128, D])
        gate_bias = sb("gate_bias", [128, E])
        router = sb("router", [128, 2 * E + 1])
        up0 = sb("up0", [128, 2, L0_TILES * 128])
        down0 = sb("down0", [128, L0_TILES, D])
        up1 = sb("up1", [128, 2, L1_ROWS])
        down1 = sb("down1", [128, L1_TILES, D])
        spread0 = sb("spread0", [GATE_ROWS, E, 128], BF16)
        spread1 = sb("spread1", [GATE_ROWS, L1_TILES, 128], BF16)
        identb = sb("identb", [128, 128], BF16)
        fused = sb("fused", [128, 2 * D + 2])
        least_lead = sb("least_lead", [128, E, E])
        w_interp = sb("w_interp", [128, PAIRS * 2])
        penalty = sb("penalty", [128, 3, CHUNK])
        any_col = sb("any_col", [128, 1])
        any_diag = sb("any_diag", [HALF, HALF])
        ones = sb("ones", [128, 128])
        any_row = sb("any_row", [128, HALF])
        minus_half = sb("minus_half", [128, PAIRS])
        euler = sb("euler", [128, PP, E + 1])

        rows = sb("rows", [128, PAIRS, 2, BLOCKS, D])
        cols = sb("cols", [128, PAIRS, 2, BLOCKS, BR])
        sel = sb("sel", [2 * S, PAIRS, 2, D])
        A0, A1, qk_bias, qb_bias = (fused[:, a:b] for a, b in [
            (0, D), (D, 2 * D), (2 * D, 2 * D + 1), (2 * D + 1, 2 * D + 2)])
        bqk = sb("bqk", [128, 1])
        masked = sb("masked", [128, 1])
        x_in = sb("x_in", [128, PAIRS, D])
        x = sb("x", [128, PAIRS, D])
        x_out = sb("x_out", [128, PAIRS, D])
        stats = sb("stats", [128, PAIRS, 6])
        mv = sb("mv", [128, PAIRS, 2])
        var = sb("var", [128, PAIRS])
        rstd = sb("rstd", [128, PAIRS])
        xn = sb("xn", [128, PAIRS, D])
        xnT = sb("xnT", [128, GT])
        qk = sb("qk", [128, GT])
        kcT = sb("kcT", [128, GT])
        vc = sb("vc", [128, PAIRS, D])
        late = sb("late", [128, 4, GT])
        selT = [late[:, p, 0:2 * PR] for p in range(PARTS)]
        qsT = late[:, 2:4, :].rearrange("p a (k t) -> p (a k) t", k=4)
        onT, c2sT, gate, diff = (late[:, i, :] for i in range(4))
        lead = [late[:, 1, p * PT:p * PT + PP * E * E].rearrange("p (s e j) -> p s e j", s=PP, e=E)
                for p in range(PARTS)]
        s2 = sb("s2", [128, PAIRS * 2, S])
        s2max = sb("s2max", [128, PAIRS * 2])
        s2sum = sb("s2sum", [128, PAIRS * 2])
        coef = sb("coef", [128, PAIRS * 2])
        p2 = sb("p2", [128, PAIRS, PAIR])
        p2T = sb("p2T", [128, GT])
        s2cT = sb("s2cT", [128, GT])
        top = sb("top", [128, PAIRS])
        ntop = sb("ntop", [128, PAIRS])
        minus_qb = sb("minus_qb", [128, PAIRS])
        total = sb("total", [128, PAIRS, 3])
        tops = sb("tops", [128, 3])
        rtotal = sb("rtotal", [128, PAIRS])
        work = sb("work", [128, S2 + BLOCKS * PAIR])
        prob = work[:, 0:S2].rearrange("p (c n) -> p c n", c=3)
        pT = work[:, S2:S2 + BLOCKS * PAIR].rearrange("p (j t) -> p j t", j=BLOCKS)
        mask_u8 = work[:, S2:].bitcast(U8)[:, 0:S2]
        sg, hu, h = (work[:, at:at + DEPTH * PR].rearrange("p (k t) -> p k t", k=DEPTH)
                     for at in (0, DEPTH * PR, S2))
        assert 2 * DEPTH * PR <= S2
        on = sb("on", [128, PAIRS, D])
        lg = sb("lg", [128, PAIRS, E + 1])
        lmax = sb("lmax", [128, PAIRS])
        lsum = sb("lsum", [128, PAIRS, 2])
        share = sb("share", [128, PAIRS, E])
        key = sb("key", [128, PAIRS, E])
        rank = sb("rank", [128, PAIRS, E])
        gates = sb("gates", [128, PAIRS, E + 1])
        rest = sb("rest", [128, PAIRS, E + 1])
        gates3 = sb("gates3", [128, PAIRS, GATE_ROWS], BF16)
        gatesT = sb("gatesT", [GATE_ROWS, GT], BF16)
        yT = sb("yT", [128, GT])

        ps = ctx.enter_context(nc.psum_tensor("ps", [128, 8, BANK], F32))

        def ring(name):
            return ps[:, RING[AT[name] % 3], :]

        scores = ps[:, 0:3, 0:CHUNK]
        fused_bank = ps[:, SUM_BANKS[0], 0:2 * D + 3]

        w_in = sem("w_in")
        bv_in = sem("bv_in")
        consts_in = sem("consts_in")
        mask_in = sem("mask_in")
        experts_in = sem("experts_in")
        x_loaded, x_taken = sem("x_loaded"), sem("x_taken")
        sel_loaded = sem("sel_loaded")
        rows_loaded = [sem(f"rows_loaded{s}") for s in range(PAIRS)]
        cols_loaded = [sem(f"cols_loaded{s}") for s in range(PAIRS)]
        zeroed = sem("zeroed")
        setup = sem("setup")
        bqk_done = sem("bqk_done")
        fused_filled, fused_done = sem("fused_filled"), sem("fused_done")
        penalty_zeroed, penalty_done = sem("penalty_zeroed"), sem("penalty_done")
        any_filled = sem("any_filled")
        ring_filled = sem("ring_filled")
        ring_free = [sem(f"ring_free{b}") for b in range(3)]
        scored = sem("scored")
        max_done = sem("max_done")
        exp_done = sem("exp_done")
        summed = sem("summed")
        on_done = sem("on_done")
        var_done, rstd_done = sem("var_done"), sem("rstd_done")
        xn_done = sem("xn_done")
        s2_sub, s2_exp, s2_mix = sem("s2_sub"), sem("s2_exp"), sem("s2_mix")
        diff_done = sem("diff_done")
        mixed = sem("mixed")
        lg_sub = sem("lg_sub")
        lg_exp = [sem(f"lg_exp{p}") for p in range(PARTS)]
        gates_done = sem("gates_done")
        gu_filled = sem("gu_filled")
        silu_done = sem("silu_done")
        h_done = sem("h_done")
        y_done, y_copied = sem("y_done"), sem("y_copied")
        apart = sem("apart")
        dve_step = sem("dve_step")
        stored = sem("stored")
        out_free = sem("out_free")

        N_LOADS = dict(w=2, consts=5, mask=2, experts=7)

        def base(name):
            return 0 if name in EARLY_FILLS else 1

        def filled(g, name):
            return g * FILLS + (base(name) * FILLS + AT[name] + 1)

        def await_bank(eng, g, name):
            k = AT[name]
            eng.wait_ge(ring_free[k % 3], g * USES[k % 3] + (base(name) * USES[k % 3] + k // 3 + 1))

        def await_copy(eng, g, name):
            k = AT[name]
            eng.wait_ge(ring_free[k % 3], g * USES[k % 3] + (base(name) * USES[k % 3] + k // 3 + 2))

        def chunks_due(g, step, c):
            return 3 * due(g, *step) - (2 - c)

        def await_ring(eng, g, fill, copied):
            k = AT[fill]
            counts = {k % 3: base(fill) * USES[k % 3] + k // 3 + 1}
            for name in copied:
                k = AT[name]
                counts[k % 3] = max(counts.get(k % 3, 0), base(name) * USES[k % 3] + k // 3 + 2)
            for bank, count in sorted(counts.items()):
                eng.wait_ge(ring_free[bank], g * USES[bank] + count)

        def await_inner(eng, g, layer, part, t):
            if routed(layer, t):
                await_copy(eng, g, f"g{layer}{part}.{t}")
            else:
                eng.wait_ge(h_done, g * len(UNROUTED) + UNROUTED.index((layer, part, t)) + 1)

        def emptied(name):
            return ring_free[AT[name] % 3]

        def part_of(tile, p):
            return tile[:, p * PT:(p + 1) * PT]

        def real(tile):
            return tile.rearrange("p (n q) -> p n q", q=HALF)[:, :, 0:S]

        def pairs(p):
            return range(p * PP, (p + 1) * PP)

        def pslice(p):
            return slice(p * PP, (p + 1) * PP)

        lo, hi, _ = interpolation()
        assert all(hi == lo + 1)
        PERIOD = next(r for r in range(1, S) if all(lo[i + r] - lo[i] == lo[r] - lo[0] for i in range(S - r)))
        STEP = int(lo[PERIOD] - lo[0])
        assert S % PERIOD == 0 and STEP * (S // PERIOD) == S2

        x_dram = d["x"].rearrange("(p h) s e -> h s p e", h=2)
        out_dram = d["out"].rearrange("(p h) s e -> h s p e", h=2)
        sel_dram = d["ctx"].rearrange("(p h) n e -> h n p e", h=2)
        rows_dram = d["ctx"].rearrange("(p h) (r j) e -> p r h (j e)", h=2, j=BLOCKS)
        cols_dram = d["ctxT"].rearrange("(p h) e n -> p e h n", h=2)

        def for_all(eng, step, skipped=None, at_start=None, at_turn=None, at_end=None):
            def turn(g, normal=True, early=True):
                if at_turn:
                    at_turn(g)
                for this in SCHEDULE:
                    if this in EARLY and early:
                        step(g + 1, *this)
                    elif this not in EARLY and normal:
                        step(g, *this)
                    elif skipped:
                        skipped(g + 1 if this in EARLY else g, *this)

            turn(-1, normal=False)
            if at_start:
                at_start()
            with eng.Fori(0, GROUPS - 1) as g:
                turn(g)
                if at_end:
                    at_end()
            turn(GROUPS - 1, early=False)

        block = ctx.enter_context(nc.Block())

        @block.sync
        def _(sp):
            def load_tokens(g):
                if not isinstance(g, int):
                    sp.wait_ge(x_taken, g * PARTS)
                for half in range(2):
                    sp.dma_start(x_in[HALF * half:HALF * half + S, :, :],
                                 x_dram[half, :, bass.ds(g * PAIRS, PAIRS), :]).then_inc(x_loaded, 16)

            def load_selected(g):
                if not isinstance(g, int):
                    sp.wait_ge(ring_filled, filled(g - 1, "sel1"))
                n = 2 * S // PERIOD
                for r in range(PERIOD):
                    sp.dma_start(
                        sel[r:r + PERIOD * (n - 1) + 1:PERIOD, :, :, :].rearrange("q p w e -> q p (w e)"),
                        bass.AP(d["ctx"].tensor, int(lo[r]) * D + g * PAIRS * 2 * S2 * D,
                                [[STEP * D, n], [2 * S2 * D, PAIRS], [1, 2 * D]]),
                    ).then_inc(sel_loaded, 16)

            def load_cols(g, s):
                if not isinstance(g, int):
                    sp.wait_ge(scored, chunks_due(g - 1, ("scores", 1, s), 2))
                sp.dma_start(cols[:, s].rearrange("p h j r -> p h (j r)"),
                             cols_dram[bass.ds(g * PAIRS + s, 1)].rearrange("a e h n -> (a e) h n")
                             ).then_inc(cols_loaded[s], 16)

            def load_rows(g, s):
                if not isinstance(g, int):
                    sp.wait_ge(summed, due(g - 1, "sum", 1, s))
                src = rows_dram[bass.ds(g * PAIRS + s, 1)].rearrange("a r h n -> (a r) h n")
                dst = rows[:, s].rearrange("p h j e -> p h (j e)")
                sp.dma_start(dst[0:MAIN], src[0:MAIN]).then_inc(rows_loaded[s], 16)
                sp.dma_start(dst[MAIN:BR], src[MAIN:BR]).then_inc(rows_loaded[s], 16)

            def store(g):
                await_copy(sp, g, "yT11")
                for half in range(2):
                    sp.dma_start(out_dram[half, :, bass.ds(g * PAIRS, PAIRS), :],
                                 x_out[HALF * half:HALF * half + S, :, :]).then_inc(stored, 16)
                sp.wait_ge(stored, 32 * g + 32)
                sp.sem_inc(out_free, 1)

            sp.sem_inc(out_free, 1)
            sp.wait_ge(zeroed, 1)
            load_tokens(0)
            load_cols(0, 0)
            load_rows(0, 0)
            for dst, src in [
                (gate_bias[:, :], d["gate_bias"].partition_broadcast(128)),
                (router[:, :], d["router"]),
                (identb[:, :], d["identb"]),
                (least_lead[:, :, :].rearrange("p e j -> p (e j)"), d["least_lead"].partition_broadcast(128)),
                (w_interp[:, :], d["w_interp"]),
            ]:
                sp.dma_start(dst, src).then_inc(consts_in, 16)
            load_cols(0, 1)
            load_selected(0)
            load_rows(0, 1)
            for s in range(2, PAIRS):
                load_cols(0, s)
                load_rows(0, s)
            for dst, src in [
                (up0[:, :, :], d["up0"]), (down0[:, :, :], d["down0"]), (spread0[:, :, :], d["spread0"]),
                (up1[:, :, :], d["up1"]), (down1[:, 0:L1_TILES - 1, :], d["down1"][:, 0:L1_TILES - 1, :]),
                (down1[0:L1_ROWS % 128, L1_TILES - 1, :], d["down1"][0:L1_ROWS % 128, L1_TILES - 1, :]),
                (spread1[:, :, :], d["spread1"]),
            ]:
                sp.dma_start(dst, src).then_inc(experts_in, 16)
            with sp.Fori(1, GROUPS) as g:
                load_tokens(g)
                load_selected(g)
                for s in range(PAIRS):
                    load_cols(g, s)
                    load_rows(g, s)
                store(g - 1)
            store(GROUPS - 1)

        @block.gpsimd
        def _(pool):
            for tile, value in [(x_in[:, :, :], 0.0), (ones[:, :], 1.0), (minus_half[:, :], -0.5),
                                (masked[:, :], MASKED), (euler[:, :, :], EULER), (late[:, 2:4, :], 0.0),
                                (p2[:, :, :], 0.0), (gates3[:, :, :], 0.0), (yT[:, :], 0.0)]:
                pool.memset(tile, value).then_inc(zeroed, 1)
            pool.wait_ge(w_in, 16 * N_LOADS["w"])
            pool.tensor_tensor(bqk[:, :], Bc["bq_c"], Bc["bk_s"], ALU.mult).then_inc(bqk_done, 1)
            pool.wait_ge(zeroed, N_ZEROED)

            def step(g, kind, *at):
                if kind == "stats":
                    n, p = at
                    pool.wait_ge(var_done, due(g, kind, *at))
                    pool.tensor_tensor(rstd[:, pslice(p)], var[:, pslice(p)], minus_half[:, pslice(p)], ALU.pow
                                       ).then_inc(rstd_done, 1)
                elif kind == "lg" and at[1] == 1:
                    layer, p = at
                    n = E + layer
                    pool.wait_ge(lg_sub, due(g, kind, *at))
                    pool.tensor_tensor(lg[:, pslice(p), 0:n], euler[:, :, 0:n], lg[:, pslice(p), 0:n], ALU.pow
                                       ).then_inc(lg_exp[1], 1)
                elif kind == "gate":
                    p, = at
                    await_copy(pool, g, f"s2c{p}")
                    await_copy(pool, g, f"c2s{p}")
                    pool.tensor_tensor(part_of(diff, p), part_of(c2sT, p), part_of(s2cT, p), ALU.subtract
                                       ).then_inc(diff_done, 1)

            for_all(pool, step)

        @block.tensor
        def _(pe):
            pe.wait_ge(w_in, 16 * N_LOADS["w"])
            pe.wait_ge(zeroed, N_ZEROED)
            pe.wait_ge(bqk_done, 1)
            for first, n, lhs, rhs in [(0, D, W["Wqc"], W["Wks"]), (D, D, W["wiT"], W["wiT"]),
                                       (2 * D, 1, W["Wks"], Bc["bq_c"]), (2 * D + 1, 1, ones[:, :], bqk[:, :]),
                                       (2 * D + 2, 1, W["Wqc"], Bc["bk_s"])]:
                mm = pe.matmul(fused_bank[:, first:first + n], lhs, rhs, start=True, stop=True)
            mm.then_inc(fused_filled, 1)
            pe.wait_ge(setup, 2)
            pe.matmul(ps[:, SUM_BANKS[1], 0:HALF], ones[0:S, :], any_diag[0:S, :], start=True, stop=True
                      ).then_inc(any_filled, 1)
            pe.wait_ge(fused_done, 2)
            pe.sem_inc(ring_filled, FIRST_EARLY)
            for b in range(3):
                pe.sem_inc(ring_free[b], 1 + len(range(b, FIRST_EARLY, 3)))

            def skipped(g, *this):
                for name in fills_of(*this):
                    if isinstance(g, int) and g == -1 and AT[name] < FIRST_EARLY:
                        continue
                    await_bank(pe, g, name)
                    pe.wait_ge(ring_filled, filled(g, name) - 1)
                    pe.sem_inc(ring_filled, 1)
                    pe.sem_inc(emptied(name), 1)

            def transposes(g, name, tiles, rows_out=128):
                await_bank(pe, g, name)
                for k, t in enumerate(tiles):
                    n = t.shape[0]
                    mm = pe.transpose(ring(name)[0:rows_out, k * n:(k + 1) * n], t, W["ident"][0:n, 0:n])
                mm.then_inc(ring_filled, 1)

            def project(g, name, weight, source, of):
                await_ring(pe, g, name, copied=[of])
                pe.matmul(ring(name)[:, 0:source.shape[1]], weight, source, start=True, stop=True
                          ).then_inc(ring_filled, 1)

            def pair_scores(g, layer, s):
                if layer == 0:
                    pe.wait_ge(cols_loaded[s], 16 * g + 16)
                    await_copy(pe, g, f"qk{s // PP}")
                else:
                    await_copy(pe, g, f"qw{s // PP}")
                if s == 0 and not (isinstance(g, int) and g == 0 and layer == 0):
                    await_inner(pe, g if layer else g - 1, *[tile for tile in TILES if tile[0] != layer][-1])
                for c in range(3):
                    for half in range(2):
                        mm = pe.matmul(ps[HALF * half:HALF * half + HALF, c, 0:CHUNK],
                                       qk[:, s * PAIR + HALF * half:s * PAIR + HALF * half + HALF],
                                       cols[:, s, half, 4 * c:4 * c + 4, :], start=True, stop=True)
                    mm.then_inc(scored, 1)

            def turn_probs(g, layer, s):
                flat = prob[:, :, :].rearrange("p c n -> p (c n)")
                for c in range(3):
                    pe.wait_ge(exp_done, chunks_due(g, ("scores", layer, s), c))
                    transposes(g, f"turn{layer}{s}.{c}",
                               [flat[:, (4 * c + k) * BR:(4 * c + k + 1) * BR] for k in range(4)], rows_out=BR)

            def context_sum(g, layer, s):
                if layer == 0:
                    pe.wait_ge(rows_loaded[s], 32 * g + 32)
                bank = ps[:, SUM_BANKS[s % 2], 0:D]
                if s == 1 and layer == 0:
                    pe.wait_ge(setup, N_SETUP)
                if s >= 2:
                    pe.wait_ge(on_done, due(g, "sum", layer, s - 2))
                for j in range(BLOCKS):
                    if j % 4 == 0:
                        await_copy(pe, g, f"turn{layer}{s}.{j // 4}")
                    for half in range(2):
                        mm = pe.matmul(bank[HALF * half:HALF * half + HALF, :],
                                       pT[0:BR, j, HALF * half:HALF * half + HALF],
                                       rows[0:BR, s, half, j, :], start=(j == 0), stop=(j == BLOCKS - 1))
                mm.then_inc(summed, 1)

            def tile_products(g, layer, p, t):
                up, spread = [(up0, spread0), (up1, spread1)][layer]
                M, k = tile_rows(layer, t), TILES.index((layer, p, t))
                if k >= DEPTH and TILES[k - DEPTH][0] == layer:
                    await_inner(pe, g, *TILES[k - DEPTH])
                if k == 0:
                    pe.wait_ge(experts_in, 16 * N_LOADS["experts"])
                xs = real(part_of(xnT, p))
                bank = ps[0:M, k % DEPTH, :]
                await_copy(pe, g, f"xnT{2 * layer + 1}{p}")
                pe.matmul(bank[:, 0:PR], up[:, 0, t * 128:t * 128 + M], xs, start=True, stop=True)
                pe.matmul(bank[:, PR:2 * PR], up[:, 1, t * 128:t * 128 + M], xs, start=True, stop=True
                          ).then_inc(gu_filled, 1)
                if routed(layer, t):
                    name = f"g{layer}{p}.{t}"
                    await_ring(pe, g, name, copied=[f"gt{layer}{p}"])
                    pe.matmul(ring(name)[0:M, 0:PR], spread[:, t, 0:M], real(part_of(gatesT, p)),
                              start=True, stop=True).then_inc(ring_filled, 1)

            def down_product(g, layer, p, t):
                down = [down0, down1][layer]
                M = tile_rows(layer, t)
                first, last = (("down", layer, p, t) == which[layer, p] for which in (FIRST_DOWN, LAST_DOWN))
                if first:
                    pe.wait_ge(on_done, due(g, "sum", layer, PP + p))
                await_inner(pe, g, layer, p, t)
                mm = pe.matmul(ps[:, SUM_BANKS[p], 0:PR], down[0:M, t, :], h[0:M, in_flight(layer, p, t), :],
                               start=first, stop=last)
                if last:
                    mm.then_inc(y_done, 1)

            def step(g, kind, *at):
                if kind == "sel":
                    p, = at
                    pe.wait_ge(sel_loaded, (g + 1) * 16 * PERIOD)
                    transposes(g, f"sel{p}", [sel[:, s, k, :] for s in pairs(p) for k in range(2)])
                elif kind == "qs":
                    p, = at
                    project(g, f"qs{p}", W["WqsT"], selT[p], f"sel{p}")
                elif kind == "xnT":
                    n, p = at
                    pe.wait_ge(xn_done, due(g, "norm", n, p))
                    transposes(g, f"xnT{n}{p}", [xn[:, s, :] for s in pairs(p)])
                elif kind == "kc":
                    project(g, f"kc{at[0]}", W["WkcT"], part_of(xnT, at[0]), f"xnT0{at[0]}")
                elif kind == "qk":
                    project(g, f"qk{at[0]}", A0, part_of(xnT, at[0]), f"xnT0{at[0]}")
                elif kind == "vc":
                    p, = at
                    await_ring(pe, g, f"vc{p}", copied=[f"xnT0{p}"])
                    for k, s in enumerate(pairs(p)):
                        mm = pe.matmul(ring(f"vc{p}")[:, k * (D + 1):(k + 1) * (D + 1)], xnT[:, s * PAIR:(s + 1) * PAIR],
                                       WvcT_qb, start=True, stop=True)
                    mm.then_inc(ring_filled, 1)
                elif kind == "s2":
                    p, = at
                    name = f"s2{p}"
                    await_ring(pe, g, name, copied=[f"qs{p}", f"kc{p}"])
                    for k in range(2 * PP):
                        s = p * PP + k // 2
                        mm = pe.matmul(ring(name)[:, k * 128:(k + 1) * 128], qsT[:, 2 * PP * p + k, :],
                                       kcT[:, s * PAIR:(s + 1) * PAIR], start=True, stop=True)
                    mm.then_inc(ring_filled, 1)
                elif kind == "p2":
                    p, = at
                    pe.wait_ge(s2_mix, due(g, "s2mix", p))
                    transposes(g, f"p2{p}", [p2[:, s, :] for s in pairs(p)])
                elif kind == "s2c":
                    p, = at
                    await_ring(pe, g, f"s2c{p}", copied=[f"p2{p}", f"vc{p}"])
                    for k, s in enumerate(pairs(p)):
                        mm = pe.matmul(ring(f"s2c{p}")[:, k * D:(k + 1) * D], vc[:, s, :],
                                       p2T[:, s * PAIR:(s + 1) * PAIR], start=True, stop=True)
                    mm.then_inc(ring_filled, 1)
                elif kind == "scores":
                    pair_scores(g, *at)
                elif kind == "turn":
                    turn_probs(g, *at)
                elif kind == "sum":
                    context_sum(g, *at)
                elif kind == "on":
                    layer, p = at
                    pe.wait_ge(on_done, due(g, "sum", layer, PP * p + PP - 1))
                    transposes(g, f"on{layer}{p}", [on[:, s, :] for s in pairs(p)])
                elif kind == "c2s":
                    project(g, f"c2s{at[0]}", W["WvsT"], part_of(onT, at[0]), f"on0{at[0]}")
                elif kind == "gate":
                    p, = at
                    out = ring(f"gate{p}")[:, 0:PT]
                    await_ring(pe, g, f"gate{p}", copied=[f"s2c{p}", f"c2s{p}"])
                    pe.matmul(out, W["WgaT"], part_of(c2sT, p), start=True, stop=False)
                    pe.matmul(out, W["WgbT"], part_of(s2cT, p), start=False, stop=True).then_inc(ring_filled, 1)
                elif kind == "dx":
                    p, = at
                    pe.wait_ge(mixed, due(g, "mix", p))
                    transposes(g, f"dx{p}", [gate[:, s * PAIR:(s + 1) * PAIR] for s in pairs(p)])
                elif kind == "lg":
                    layer, p = at
                    weight, n = [(router[:, 0:E], E), (router[:, E:2 * E + 1], E + 1)][layer]
                    name = f"lg{layer}{p}"
                    await_ring(pe, g, name, copied=[f"xnT{2 * layer + 1}{p}"])
                    for k, s in enumerate(pairs(p)):
                        mm = pe.matmul(ring(name)[:, k * n:(k + 1) * n], xnT[:, s * PAIR:(s + 1) * PAIR], weight,
                                       start=True, stop=True)
                    mm.then_inc(ring_filled, 1)
                elif kind == "gt":
                    layer, p = at
                    name = f"gt{layer}{p}"
                    pe.wait_ge(gates_done, due(g, "gates", layer, p))
                    await_bank(pe, g, name)
                    for k, s in enumerate(pairs(p)):
                        mm = pe.transpose(ring(name).bitcast(BF16)[0:GATE_ROWS, k * 128:(k + 1) * 128],
                                          gates3[:, s, :], identb[:, :])
                    mm.then_inc(ring_filled, 1)
                elif kind == "tile":
                    tile_products(g, *at)
                elif kind == "down":
                    down_product(g, *at)
                elif kind == "yT":
                    layer, p = at
                    pe.wait_ge(y_copied, due(g, "y", layer, p))
                    transposes(g, f"yT{layer}{p}", [yT[:, s * PAIR:(s + 1) * PAIR] for s in pairs(p)])
                elif kind == "qw":
                    project(g, f"qw{at[0]}", A1, part_of(xnT, at[0]), f"xnT2{at[0]}")
                elif kind == "o1":
                    p, = at
                    await_ring(pe, g, f"o1{p}", copied=[f"on1{p}"])
                    for k, s in enumerate(pairs(p)):
                        bank = ring(f"o1{p}")[:, k * D:(k + 1) * D]
                        mm = pe.matmul(bank, onT[:, s * PAIR:(s + 1) * PAIR], W["wi"], start=True, stop=True)
                    mm.then_inc(ring_filled, 1)

            for_all(pe, step, skipped)

        @block.scalar
        def _(act):
            def load_mask(half):
                act.dma_start(mask_u8[HALF * half:HALF * half + S, :], d["mask"]).then_inc(mask_in, 16)

            load_mask(0)
            act.dma_start(w[:, 0:len(W_NAMES) * D], d["w"]).then_inc(w_in, 16)
            act.dma_start(bias[:, :], d["bias"]).then_inc(w_in, 16)
            load_mask(1)
            act.dma_start(bv_c_row[:, :], d["bv_c"].partition_broadcast(128)).then_inc(bv_in, 16)

            def penalty_half(half):
                q = slice(HALF * half, HALF * half + S)
                act.activation(penalty[q, :, :].rearrange("p c (j r) -> p (c j) r", j=4),
                               mask_u8[q, :].rearrange("p (r j) -> p j r", j=BLOCKS),
                               ACT.Identity, bias=masked[q, 0:1], scale=-MASKED).then_inc(penalty_done, 1)

            act.wait_ge(zeroed, N_ZEROED)
            act.wait_ge(penalty_zeroed, 1)
            act.wait_ge(mask_in, 16 * N_LOADS["mask"])
            penalty_half(0)
            act.wait_ge(fused_filled, 1)
            act.copy(fused[:, :], fused_bank[:, 0:2 * D + 2]).then_inc(fused_done, 1)
            act.copy(qb_weight, fused_bank[:, 2 * D + 2:2 * D + 3]).then_inc(fused_done, 1)
            penalty_half(1)

            def copy(g, name, out, bias=None):
                act.wait_ge(ring_filled, filled(g, name))
                source = ring(name)[0:out.shape[0], 0:out.shape[1]]
                if bias is None:
                    act.copy(out, source).then_inc(emptied(name), 1)
                else:
                    act.activation(out, source, ACT.Identity, bias=bias).then_inc(emptied(name), 1)

            def step(g, kind, *at):
                if kind == "sel":
                    copy(g, f"sel{at[0]}", selT[at[0]])
                elif kind == "qs":
                    p, = at
                    act.wait_ge(ring_filled, filled(g, f"qs{p}"))
                    act.activation(real(late[:, 2 + p, :]), ring(f"qs{p}")[:, 0:2 * PR].rearrange("p (n q) -> p n q", q=S),
                                   ACT.Identity, bias=Bc["bq_s"]).then_inc(emptied(f"qs{p}"), 1)
                elif kind == "xnT":
                    n, p = at
                    copy(g, f"xnT{n}{p}", part_of(xnT, p))
                elif kind == "scores":
                    layer, s = at
                    act.wait_ge(max_done, due(g, kind, *at))
                    source = scores if layer == 0 else prob
                    shift = (ntop if layer == 0 else top)[:, s:s + 1]
                    for c in range(3):
                        act.activation(prob[:, c, :], source[:, c, :], ACT.Exp, bias=shift,
                                       accum_out=total[:, s, c:c + 1]).then_inc(exp_done, 1)
                elif kind == "s2exp":
                    p, = at
                    both = s2[:, 2 * PP * p:2 * PP * (p + 1), :]
                    act.wait_ge(s2_sub, due(g, "s2", p))
                    act.activation(both, both, ACT.Exp).then_inc(s2_exp, 1)
                elif kind == "lg" and at[1] == 0:
                    layer, p = at
                    both = lg[:, pslice(p), 0:E + layer]
                    act.wait_ge(lg_sub, due(g, kind, *at))
                    act.activation(both, both, ACT.Exp).then_inc(lg_exp[0], 1)
                elif kind == "p2":
                    copy(g, f"p2{at[0]}", part_of(p2T, at[0]))
                elif kind == "s2c":
                    copy(g, f"s2c{at[0]}", part_of(s2cT, at[0]))
                elif kind == "turn":
                    layer, s = at
                    for c in (0, 1):
                        copy(g, f"turn{layer}{s}.{c}", pT[0:BR, 4 * c:4 * c + 4, :].rearrange("p j t -> p (j t)"))
                elif kind == "on" and at[0] == 0:
                    copy(g, f"on0{at[1]}", part_of(onT, at[1]))
                elif kind == "gate":
                    p, = at
                    act.wait_ge(ring_filled, filled(g, f"gate{p}"))
                    act.activation(part_of(gate, p), ring(f"gate{p}")[:, 0:PT], ACT.Tanh, bias=half_bg[:, 0:1],
                                   scale=0.5).then_inc(emptied(f"gate{p}"), 1)
                elif kind == "tile":
                    layer, p, t = at
                    M, k = tile_rows(layer, t), in_flight(layer, p, t)
                    act.wait_ge(gu_filled, due(g, kind, *at))
                    act.activation(sg[0:M, k, :], ps[0:M, k, 0:PR], ACT.Silu).then_inc(silu_done, 1)
                elif kind == "y":
                    layer, p = at
                    act.wait_ge(y_done, due(g, kind, *at))
                    act.copy(real(part_of(yT, p)), ps[:, SUM_BANKS[p], 0:PR].rearrange("p (n q) -> p n q", q=S)
                             ).then_inc(y_copied, 1)

            for_all(act, step)

        @block.vector
        def _(dve):
            def wait_apart(semaphore, value):
                dve.wait_ge(semaphore, value)
                dve.sem_inc(apart, 1)

            class Steps:
                def __init__(self, semaphore):
                    self.semaphore, self.g, self.per, self.n = semaphore, 0, 0, 0

                def start(self, g):
                    self.g, self.per, self.n = g, DVE_STEPS, DVE_EARLY

                def step(self, instruction):
                    instruction.then_inc(self.semaphore, 1)
                    self.n += 1
                    dve.wait_ge(self.semaphore, self.g * self.per + self.n)

                def step_apart(self, instruction):
                    instruction.then_inc(self.semaphore, 1)
                    self.n += 1
                    wait_apart(self.semaphore, self.g * self.per + self.n)

            own = Steps(dve_step)

            dve.memset(penalty[:, :, :], 0.0).then_inc(penalty_zeroed, 1)
            first = Steps(setup)
            dve.wait_ge(mask_in, 16 * N_LOADS["mask"])
            first.step(dve.tensor_reduce(any_col[0:S, :], mask_u8[0:S, :], X, ALU.max))
            dve.wait_ge(w_in, 16 * N_LOADS["w"])
            first.step(dve.tensor_scalar(any_diag[0:S, :], W["ident"][0:S, 0:HALF], any_col[0:S, 0:1], None,
                                         ALU.mult))

            def rest_of_setup():
                assert own.n == DVE_EARLY, own.n
                first.step(dve.tensor_scalar(half_bg[:, :], Bc["bg"], 0.5, None, ALU.mult))
                dve.wait_ge(any_filled, 1)
                first.step(dve.tensor_copy(any_row[:, :], ps[:, SUM_BANKS[1], 0:HALF]))
                dve.wait_ge(penalty_done, 2)
                dve.wait_ge(consts_in, 16 * N_LOADS["consts"])
                assert first.n == N_SETUP, first.n

            def wait_filled(g, name):
                dve.wait_ge(ring_filled, filled(g, name))

            def as_pairs(name):
                return ring(name)[:, 0:PT].rearrange("p (s e) -> p s e", s=PP)

            def add_to_x(g, name, p):
                wait_filled(g, name)
                dve.tensor_tensor(x[:, pslice(p), :], x[:, pslice(p), :], as_pairs(name), ALU.add
                                  ).then_inc(emptied(name), 1)
                await_copy(dve, g, name)

            def halves():
                return [slice(HALF * h, HALF * h + HALF) for h in range(2)]

            def small_scores(g, p):
                name = f"s2{p}"
                span = slice(2 * PP * p, 2 * PP * (p + 1))
                wait_filled(g, name)
                blocks = ring(name).rearrange("p (k t) -> p k t", k=2 * PP)
                for hs in halves():
                    ins = dve.tensor_copy(s2[hs, span, :], blocks[hs, :, hs.start:hs.start + S])
                ins.then_inc(emptied(name), 1)
                await_copy(dve, g, name)
                own.step(dve.tensor_reduce(s2max[:, span], s2[:, span, :], X, ALU.max))
                dve.tensor_tensor(s2[:, span, :], s2[:, span, :],
                                  s2max[:, span].unsqueeze(2).to_broadcast([128, 2 * PP, S]),
                                  ALU.subtract).then_inc(s2_sub, 1)

            def small_mix(g, p):
                span = slice(2 * PP * p, 2 * PP * (p + 1))
                dve.wait_ge(s2_exp, due(g, "s2exp", p))
                own.step(dve.tensor_reduce(s2sum[:, span], s2[:, span, :], X, ALU.add))
                own.step(dve.reciprocal(coef[:, span], s2sum[:, span]))
                own.step(dve.tensor_tensor(coef[:, span], coef[:, span], w_interp[:, span], ALU.mult))
                own.step(dve.tensor_tensor(s2[:, span, :], s2[:, span, :],
                                           coef[:, span].unsqueeze(2).to_broadcast([128, 2 * PP, S]), ALU.mult))
                both = s2[:, span, :].rearrange("p (s w) k -> p s w k", w=2)
                for hs in halves():
                    ins = dve.tensor_tensor(p2[hs, pslice(p), hs.start:hs.start + S],
                                            both[hs, :, 0, :], both[hs, :, 1, :], ALU.add)
                ins.then_inc(s2_mix, 1)

            def step(g, kind, *at):
                if kind == "stats":
                    n, p = at
                    if n == 0:
                        wait_apart(x_loaded, 32 * g + 32)
                    for s in pairs(p):
                        ins = dve.bn_stats(stats[:, s, :], (x if n else x_in)[:, s, :])
                    own.step_apart(ins)
                    for s in pairs(p):
                        ins = dve.bn_aggr(mv[:, s, :], stats[:, s, :])
                    own.step(ins)
                    dve.tensor_scalar(var[:, pslice(p)], mv[:, pslice(p), 1], EPS, None, ALU.add).then_inc(var_done, 1)
                elif kind == "norm":
                    n, p = at
                    dve.wait_ge(rstd_done, due(g, "stats", n, p))
                    for s in pairs(p):
                        ins = dve.tensor_scalar(xn[:, s, :], (x if n else x_in)[:, s, :], mv[:, s, 0:1], rstd[:, s:s + 1],
                                                ALU.subtract, ALU.mult)
                    ins.then_inc(xn_done, 1)
                elif kind == "qk":
                    p, = at
                    name = f"qk{p}"
                    wait_filled(g, name)
                    dve.tensor_scalar(part_of(qk, p), ring(name)[:, 0:PT], qk_bias, SCALE, ALU.add, ALU.mult
                                      ).then_inc(emptied(name), 1)
                elif kind == "kc":
                    p, = at
                    wait_filled(g, f"kc{p}")
                    dve.tensor_scalar(part_of(kcT, p), ring(f"kc{p}")[:, 0:PT], Bc["bk_c"], SCALE, ALU.add, ALU.mult
                                      ).then_inc(emptied(f"kc{p}"), 1)
                elif kind == "vc":
                    p, = at
                    name = f"vc{p}"
                    if isinstance(g, int) and g == 0:
                        dve.wait_ge(bv_in, 16)
                    both = ring(name)[:, 0:PP * (D + 1)].rearrange("p (s e) -> p s e", s=PP)
                    wait_filled(g, name)
                    dve.tensor_scalar(minus_qb[:, pslice(p)], both[:, :, D], qb_bias, -SCALE, ALU.add, ALU.mult)
                    dve.tensor_tensor(vc[:, pslice(p), :], both[:, :, 0:D],
                                      bv_c_row[:, :].unsqueeze(1).to_broadcast([128, PP, D]), ALU.add
                                      ).then_inc(emptied(name), 1)
                    await_copy(dve, g, name)
                elif kind == "s2":
                    small_scores(g, *at)
                elif kind == "s2mix":
                    small_mix(g, *at)
                elif kind == "scores":
                    layer, s = at
                    this = (kind, *at)
                    for c in range(3):
                        if layer == 0:
                            dve.wait_ge(scored, chunks_due(g, this, c))
                            ins = dve.tensor_reduce(tops[:, c:c + 1], scores[:, c, :], X, ALU.max)
                        else:
                            wait_apart(scored, chunks_due(g, this, c))
                            ins = dve.tensor_tensor_reduce(prob[:, c, :], scores[:, c, :], penalty[:, c, :], 1.0,
                                                           LOWEST, ALU.add, ALU.max, tops[:, c:c + 1])
                    own.step(ins)
                    largest = dve.tensor_reduce(top[:, s:s + 1], tops[:, :], X, ALU.max, negate=True)
                    if layer == 0:
                        own.step(largest)
                        dve.scalar_tensor_tensor(out=ntop[:, s:s + 1], in0=top[:, s:s + 1],
                                                 scalar=minus_qb[:, s:s + 1], in1=minus_qb[:, s:s + 1],
                                                 op0=ALU.add, op1=ALU.subtract).then_inc(max_done, 1)
                    else:
                        largest.then_inc(max_done, 1)
                elif kind == "turn":
                    layer, s = at
                    name = f"turn{layer}{s}.2"
                    wait_filled(g, name)
                    dve.tensor_copy(pT[0:BR, 8:12, :].rearrange("p j t -> p (j t)"), ring(name)[0:BR, :]
                                    ).then_inc(emptied(name), 1)
                elif kind == "sum":
                    layer, s = at
                    dve.wait_ge(exp_done, chunks_due(g, ("scores", layer, s), 2))
                    own.step(dve.tensor_reduce(rtotal[:, s:s + 1], total[:, s, :], X, ALU.add))
                    own.step(dve.reciprocal(rtotal[:, s:s + 1], rtotal[:, s:s + 1]))
                    dve.wait_ge(summed, due(g, kind, *at))
                    dve.tensor_scalar(on[:, s, :], ps[:, SUM_BANKS[s % 2], 0:D], rtotal[:, s:s + 1], None, ALU.mult
                                      ).then_inc(on_done, 1)
                elif kind == "c2s":
                    p, = at
                    wait_filled(g, f"c2s{p}")
                    dve.tensor_scalar(part_of(c2sT, p), ring(f"c2s{p}")[:, 0:PT], Bc["bv_s"], None, ALU.add
                                      ).then_inc(emptied(f"c2s{p}"), 1)
                elif kind == "mix":
                    p, = at
                    out = part_of(gate, p)
                    dve.wait_ge(diff_done, due(g, "gate", p))
                    await_copy(dve, g, f"gate{p}")
                    own.step(dve.scalar_tensor_tensor(out=out, in0=out, scalar=1.0, in1=part_of(diff, p),
                                                      op0=ALU.add, op1=ALU.mult))
                    dve.scalar_tensor_tensor(out=out, in0=out, scalar=0.5, in1=part_of(s2cT, p),
                                             op0=ALU.mult, op1=ALU.add).then_inc(mixed, 1)
                elif kind == "on" and at[0] == 1:
                    p = at[1]
                    name = f"on1{p}"
                    wait_filled(g, name)
                    dve.tensor_tensor(part_of(onT, p), ring(name)[:, 0:PT], part_of(xnT, p), ALU.add
                                      ).then_inc(emptied(name), 1)
                elif kind == "dx":
                    p, = at
                    wait_filled(g, f"dx{p}")
                    dve.tensor_tensor(x[:, pslice(p), :], x_in[:, pslice(p), :], as_pairs(f"dx{p}"), ALU.add
                                      ).then_inc(emptied(f"dx{p}"), 1)
                    await_copy(dve, g, f"dx{p}")
                    dve.sem_inc(x_taken, 1)
                elif kind == "o1":
                    add_to_x(g, f"o1{at[0]}", at[0])
                elif kind == "lg":
                    layer, p = at
                    n = E + layer
                    name = f"lg{layer}{p}"
                    wait_filled(g, name)
                    z = ring(name)[:, 0:PP * n].rearrange("p (s e) -> p s e", s=PP)
                    own.step(dve.tensor_reduce(lmax[:, pslice(p)], z[:, :, 0:E], X, ALU.max))
                    if layer:
                        dve.tensor_scalar(lg[:, pslice(p), E:E + 1], z[:, :, E:E + 1], -1.0, None, ALU.mult)
                    dve.tensor_tensor(lg[:, pslice(p), 0:E], z[:, :, 0:E],
                                      lmax[:, pslice(p)].unsqueeze(2).to_broadcast([128, PP, E]),
                                      ALU.subtract).then_inc(emptied(name), 1)
                    await_copy(dve, g, name)
                    dve.sem_inc(lg_sub, 1)
                elif kind == "softmax":
                    layer, p = at
                    score = lg[:, pslice(p), 0:E]
                    sums = lsum[:, pslice(p), 0:1 + layer]
                    dve.wait_ge(lg_exp[p], g * 2 + layer + 1)
                    if layer:
                        dve.tensor_scalar(lsum[:, pslice(p), 1:2], lg[:, pslice(p), E:E + 1], 1.0, None, ALU.add)
                    own.step(dve.tensor_reduce(lsum[:, pslice(p), 0:1], score, X, ALU.add))
                    own.step(dve.reciprocal(sums, sums))
                    if layer:
                        dve.tensor_copy(gates[:, pslice(p), E:E + 1], lsum[:, pslice(p), 1:2])
                    else:
                        for s in pairs(p):
                            dve.scalar_tensor_tensor(out=key[:, s, :], in0=lg[:, s, 0:E], scalar=lsum[:, s, 0:1],
                                                     in1=gate_bias[:, :], op0=ALU.mult, op1=ALU.add)
                    own.step(dve.tensor_tensor(share[:, pslice(p), :], score, lsum[:, pslice(p), 0:1].to_broadcast([128, PP, E]),
                                               ALU.mult))
                elif kind == "rank":
                    layer, p = at
                    k = (share if layer else key)[:, pslice(p), :]
                    shape = [128, PP, E, E]
                    mine, other = k.unsqueeze(3).to_broadcast(shape), k.unsqueeze(2).to_broadcast(shape)
                    own.step(dve.tensor_tensor(lead[p], other, mine, ALU.subtract))
                    own.step(dve.tensor_tensor(lead[p], lead[p], least_lead[:, :, :].unsqueeze(1).to_broadcast(shape),
                                               ALU.is_ge))
                    own.step(dve.tensor_reduce(rank[:, pslice(p), :], lead[p], X, ALU.add))
                elif kind == "gates":
                    layer, p = at
                    n = E + layer
                    high, middle, low = (gates3[:, pslice(p), 32 * part:32 * part + n] for part in range(3))
                    left, whole = rest[:, pslice(p), 0:n], gates[:, pslice(p), 0:n]
                    for out in (whole, high):
                        ins = dve.scalar_tensor_tensor(out=out[:, :, 0:E], in0=rank[:, pslice(p), :], scalar=2.0,
                                                       in1=share[:, pslice(p), :], op0=ALU.is_lt, op1=ALU.mult)
                    if layer:
                        ins = dve.tensor_copy(high[:, :, E:n], whole[:, :, E:n])
                    own.step(ins)
                    dve.tensor_tensor(left, whole, high, ALU.subtract)
                    own.step(dve.tensor_tensor(middle, whole, high, ALU.subtract))
                    dve.tensor_tensor(low, left, middle, ALU.subtract).then_inc(gates_done, 1)
                elif kind == "gt":
                    layer, p = at
                    name = f"gt{layer}{p}"
                    wait_filled(g, name)
                    dve.tensor_copy(part_of(gatesT, p), ring(name).bitcast(BF16)[0:GATE_ROWS, 0:PT]
                                    ).then_inc(emptied(name), 1)
                elif kind == "tile":
                    layer, p, t = at
                    M, k = tile_rows(layer, t), in_flight(layer, p, t)
                    out = (hu if routed(layer, t) else h)[0:M, k, :]
                    if routed(layer, t):
                        name = f"g{layer}{p}.{t}"
                        wait_filled(g, name)
                    dve.wait_ge(silu_done, due(g, kind, *at))
                    ins = dve.tensor_tensor(out, sg[0:M, k, :], ps[0:M, k, PR:2 * PR], ALU.mult)
                    if routed(layer, t):
                        own.step(ins)
                        dve.tensor_tensor(h[0:M, k, :], out, ring(name)[0:M, 0:PR], ALU.mult
                                          ).then_inc(emptied(name), 1)
                    else:
                        ins.then_inc(h_done, 1)
                elif kind == "yT" and at[0] == 0:
                    add_to_x(g, f"yT0{at[1]}", at[1])
                elif kind == "yT":
                    p = at[1]
                    name = f"yT1{p}"
                    wait_filled(g, name)
                    if p == 0:
                        dve.wait_ge(out_free, g + 1)
                    dve.tensor_tensor(x_out[:, pslice(p), :], x[:, pslice(p), :], as_pairs(name), ALU.add
                                      ).then_inc(emptied(name), 1)
                    await_copy(dve, g, name)
                elif kind == "qw":
                    p, = at
                    name = f"qw{p}"
                    wait_filled(g, name)
                    dve.scalar_tensor_tensor(out=part_of(qk, p).rearrange("p (n q) -> p n q", q=HALF),
                                             in0=ring(name)[:, 0:PT].rearrange("p (n q) -> p n q", q=HALF),
                                             scalar=SCALE,
                                             in1=any_row[:, :].unsqueeze(1).to_broadcast([128, 2 * PP, HALF]),
                                             op0=ALU.mult, op1=ALU.mult).then_inc(emptied(name), 1)

            def start_turn(g):
                if not (isinstance(g, int) and g == -1):
                    own.start(g)

            def check_count():
                assert own.n == DVE_EARLY + DVE_STEPS, own.n - DVE_EARLY

            for_all(dve, step, at_start=rest_of_setup, at_turn=start_turn, at_end=check_count)


def kernel(**inputs):
    import ml_dtypes
    import numpy as np
    import concourse.bacc as bacc
    from concourse.bass_utils import run_bass_kernel_spmd

    a = {k: np.asarray(v) for k, v in inputs.items()}
    f32 = np.float32

    def T(name):
        return a[name].T

    def side(*blocks):
        return np.concatenate(blocks, axis=1)

    def tiles(m):
        m = np.concatenate([m, np.zeros((-len(m) % 128, m.shape[1]), m.dtype)], axis=0)
        return m.reshape(-1, 128, m.shape[1]).transpose(1, 0, 2)

    _, _, w_hi = interpolation()
    w_interp = np.zeros((128, PAIRS, 2), f32)
    for half in range(2):
        w_interp[HALF * half:HALF * half + S, :, 0] = (f32(1) - w_hi)[:, None]
        w_interp[HALF * half:HALF * half + S, :, 1] = w_hi[:, None]

    def spread(rows_of_gate, n_tiles):
        m = np.zeros((GATE_ROWS, n_tiles, 128), ml_dtypes.bfloat16)
        for r, gate in enumerate(rows_of_gate):
            for part in range(3):
                m[32 * part + gate, r // 128, r % 128] = 1
        return m

    Wg = a["L0_xattn_Wg"]
    attention = {
        "Wqc": a["L0_xattn_Wq_c"], "Wks": a["L0_xattn_Wk_s"], "WvsT": T("L0_xattn_Wv_s"),
        "WqsT": T("L0_xattn_Wq_s"), "WkcT": T("L0_xattn_Wk_c"), "WvcT": T("L0_xattn_Wv_c"),
        "WgaT": Wg[:, :D].T, "WgbT": Wg[:, D:].T, "wi": a["L1_xattn_wi"], "wiT": T("L1_xattn_wi"),
        "ident": np.eye(128, dtype=f32),
    }
    w1, w3, w2 = a["L0_ffn_w1"], a["L0_ffn_w3"], a["L0_ffn_w2"]
    gu, dn = a["L1_ffn_experts_gate_up"], a["L1_ffn_experts_down"]
    arrays = {
        "x": a["x"], "ctx": a["ctx_1024"],
        "ctxT": a["ctx_1024"].reshape(BATCH, BR, BLOCKS, D).transpose(0, 3, 2, 1).reshape(BATCH, D, S2),
        "mask": a["mask_1xSxS2_bk0"][0],
        "w": side(*[attention[n] for n in W_NAMES]),
        "bias": np.stack([a["L0_xattn_" + n] for n in B_NAMES], axis=1),
        "bv_c": a["L0_xattn_bv_c"], "gate_bias": a["L0_ffn_gate_bias"],
        "router": side(T("L0_ffn_gate_w"), T("L1_ffn_gate_w"), T("L1_ffn_shared_expert_gate_w")),
        "identb": np.eye(128, dtype=ml_dtypes.bfloat16),
        "least_lead": np.where(np.tril(np.ones((E, E)), -1) > 0, f32(0), np.finfo(f32).tiny).astype(f32).reshape(-1),
        "w_interp": w_interp.reshape(128, -1),
        "up0": np.stack([side(*[m.T for m in w1], T("L0_ffn_sw1")), side(*[m.T for m in w3], T("L0_ffn_sw3"))], axis=1),
        "down0": tiles(np.concatenate([*[m.T for m in w2], T("L0_ffn_sw2")], axis=0)),
        "spread0": spread(np.arange(E * 128) // 128, E),
        "up1": np.stack([side(*[m[:I1].T for m in gu], T("L1_ffn_shared_gate_w")),
                         side(*[m[I1:].T for m in gu], T("L1_ffn_shared_up_w"))], axis=1),
        "down1": tiles(np.concatenate([*[m.T for m in dn], T("L1_ffn_shared_down_w")], axis=0)),
        "spread1": spread(np.minimum(np.arange(L1_ROWS) // I1, E), L1_TILES),
    }
    nc = bacc.Bacc("TRN2", target_bir_lowering=False, num_devices=1)
    given, dram = {}, {}
    for name, array in arrays.items():
        given["in_" + name] = np.ascontiguousarray(array)
        dram[name] = nc.dram_tensor("in_" + name, array.shape, mybir.dt.from_np(array.dtype), kind="ExternalInput").ap()
    dram["out"] = nc.dram_tensor("out_0", (BATCH, S, D), F32, kind="ExternalOutput").ap()
    build(nc, dram)
    return run_bass_kernel_spmd(nc, [given], core_ids=[0]).results[0]["out_0"]
```
